# Optimizing a Trainium2 kernel written in Bass

```python
import numpy as np
import jax
import jax.numpy as jnp

def _softmax(x, axis=-1):
    return jax.nn.softmax(x, axis=axis)

def _gelu(x):
    return jax.nn.gelu(x, approximate=True)

def _silu(x):
    return jax.nn.silu(x)

def _sigmoid(x):
    return jax.nn.sigmoid(x)

def _layernorm(x, axis=-1, eps=1e-05):
    m = jnp.mean(x, axis=axis, keepdims=True)
    v = jnp.var(x, axis=axis, keepdims=True)
    return (x - m) / jnp.sqrt(v + eps)

def _scatter_add(tgt, idx, src, axis=0):
    return tgt.at[idx].add(src)

def _segment_sum(src, seg, n):
    return jax.ops.segment_sum(src, seg, n)
kernel_name = 'mk_gnn_preln_d4_gnn_r8_8381df'

def setup_inputs(seed: int=0):
    np.random.seed(seed)
    _w = jnp.asarray

    def _rec_inputs():
        import jax
        import jax.numpy as jnp
        _gk = jax.random.key(seed)
        x = -0.000202 + 1 * jax.random.normal(jax.random.fold_in(_gk, 1), (6250, 128), jnp.float32)
        _s = jax.random.randint(jax.random.fold_in(_gk, 2), (100000,), 0, 6250, jnp.int32)
        _d = jax.random.randint(jax.random.fold_in(_gk, 3), (100000,), 0, 6250, jnp.int32)
        _loop = jnp.arange(6250, dtype=jnp.int32)
        src = jnp.concatenate([_s, _d, _loop])
        dst = jnp.concatenate([_d, _s, _loop])
        _o = jnp.argsort(dst, stable=True)
        src = src[_o]
        dst = dst[_o]
        edge_attr_128 = -8.16379e-05 + 0.999858 * jax.random.normal(jax.random.fold_in(_gk, 11), (206250, 128), jnp.float32)
        return (x, src, dst, edge_attr_128)
    x, src, dst, edge_attr_128 = _rec_inputs()

    def _L0_gnn_setup():
        import jax, jax.numpy as jnp
        import numpy as np
        N_NODES = 6250
        N_EDGES = 100000
        DIM = 128
        key = jax.random.key(seed)
        k1, k2, k3, k4, k5, k6 = jax.random.split(key, 6)
        x = jax.random.normal(k1, (N_NODES, DIM), dtype=jnp.float32)
        edge_index = jax.random.randint(k2, (2, N_EDGES), 0, N_NODES, dtype=jnp.int64)
        W_w = jax.random.normal(k3, (DIM, DIM), dtype=jnp.float32) * (1.0 / np.sqrt(DIM))
        W_b = jax.random.normal(k4, (DIM,), dtype=jnp.float32) * 0.01
        a_w = jax.random.normal(k5, (2 * DIM, 1), dtype=jnp.float32) * (1.0 / np.sqrt(2 * DIM))
        a_b = jax.random.normal(k6, (1,), dtype=jnp.float32) * 0.01
        return {'x': x, 'edge_index': edge_index, 'W_w': W_w, 'W_b': W_b, 'a_w': a_w, 'a_b': a_b}
    _L0_gnn_all = _L0_gnn_setup()
    _L0_gnn_in = {k: v for k, v in _L0_gnn_all.items() if k in ('W_w', 'W_b', 'a_w', 'a_b')}
    del _L0_gnn_all

    def _L1_gnn_setup():
        import jax, jax.numpy as jnp
        import numpy as np
        N = 6250
        E = 100000
        D = 128
        H = 128
        LN_EPS = 1e-05

        def _layer_norm(x, gamma, beta):
            mu = jnp.mean(x, axis=-1, keepdims=True)
            var = jnp.mean(jnp.square(x - mu), axis=-1, keepdims=True)
            return (x - mu) * jax.lax.rsqrt(var + LN_EPS) * gamma + beta
        key = jax.random.key(seed)
        ks = jax.random.split(key, 9)
        s_d = 1.0 / np.sqrt(D)
        s_h = 1.0 / np.sqrt(H)
        return {'node_embeddings': jax.random.normal(ks[0], (N, D), dtype=jnp.float32), 'edge_embeddings': jax.random.normal(ks[1], (E, D), dtype=jnp.float32), 'edge_index_list': jax.random.randint(ks[2], (2, E), 0, N, dtype=jnp.int64), 'ln_gamma': jnp.ones((D,), dtype=jnp.float32), 'ln_beta': jnp.zeros((D,), dtype=jnp.float32), 'phi_w1': jax.random.normal(ks[3], (D, H), dtype=jnp.float32) * s_d, 'phi_b1': jnp.zeros((H,), dtype=jnp.float32), 'phi_w2': jax.random.normal(ks[4], (H, D), dtype=jnp.float32) * s_h, 'phi_b2': jnp.zeros((D,), dtype=jnp.float32), 'theta_w': jax.random.normal(ks[5], (D, D), dtype=jnp.float32) * s_d, 'theta_b': jnp.zeros((D,), dtype=jnp.float32)}
    _L1_gnn_all = _L1_gnn_setup()
    _L1_gnn_in = {k: v for k, v in _L1_gnn_all.items() if k in ('ln_gamma', 'ln_beta', 'phi_w1', 'phi_b1', 'phi_w2', 'phi_b2', 'theta_w', 'theta_b')}
    del _L1_gnn_all

    def _L2_gnn_setup():
        import jax, jax.numpy as jnp
        import numpy as np
        N = 12500
        E = 100000
        D = 128
        OUT = 128
        key = jax.random.key(seed)
        k = jax.random.split(key, 6)
        x = jax.random.normal(k[0], (N, D), dtype=jnp.float32)
        edge_index = jax.random.randint(k[1], (2, E), 0, N, dtype=jnp.int64)
        Wl = jax.random.normal(k[2], (D, OUT), dtype=jnp.float32) / np.sqrt(D)
        bl = jax.random.normal(k[3], (OUT,), dtype=jnp.float32) * 0.01
        Wr = jax.random.normal(k[4], (D, OUT), dtype=jnp.float32) / np.sqrt(D)
        br = jax.random.normal(k[5], (OUT,), dtype=jnp.float32) * 0.01
        return {'x': x, 'edge_index': edge_index, 'Wl': Wl, 'bl': bl, 'Wr': Wr, 'br': br}
    _L2_gnn_all = _L2_gnn_setup()
    _L2_gnn_in = {k: v for k, v in _L2_gnn_all.items() if k in ('Wl', 'bl', 'Wr', 'br')}
    del _L2_gnn_all

    def _L3_gnn_setup():
        import jax, jax.numpy as jnp
        import numpy as np
        N = 6250
        E = 100000
        IN = 128
        OUT = 32
        H = 4
        NEG_SLOPE = 0.2
        key = jax.random.key(seed)
        k1, k2, k3, k4, k5 = jax.random.split(key, 5)
        x = jax.random.normal(k1, (N, IN), dtype=jnp.float32)
        edge_index = jax.random.randint(k2, (2, E), 0, N, dtype=jnp.int32)
        W = jax.random.normal(k3, (H * OUT, IN), dtype=jnp.float32) * (1.0 / np.sqrt(IN))
        att_src = jax.random.normal(k4, (1, H, OUT), dtype=jnp.float32) * (1.0 / np.sqrt(OUT))
        att_dst = jax.random.normal(k5, (1, H, OUT), dtype=jnp.float32) * (1.0 / np.sqrt(OUT))
        bias = jnp.zeros((H * OUT,), dtype=jnp.float32)
        return {'x': x, 'edge_index': edge_index, 'W': W, 'att_src': att_src, 'att_dst': att_dst, 'bias': bias}
    _L3_gnn_all = _L3_gnn_setup()
    _L3_gnn_in = {k: v for k, v in _L3_gnn_all.items() if k in ('W', 'att_src', 'att_dst', 'bias')}
    del _L3_gnn_all
    return {'x': x, 'src': src, 'dst': dst, 'edge_attr_128': edge_attr_128, 'L0_gnn_W_w': _L0_gnn_in['W_w'], 'L0_gnn_W_b': _L0_gnn_in['W_b'], 'L0_gnn_a_w': _L0_gnn_in['a_w'], 'L0_gnn_a_b': _L0_gnn_in['a_b'], 'L1_gnn_ln_gamma': _L1_gnn_in['ln_gamma'], 'L1_gnn_ln_beta': _L1_gnn_in['ln_beta'], 'L1_gnn_phi_w1': _L1_gnn_in['phi_w1'], 'L1_gnn_phi_b1': _L1_gnn_in['phi_b1'], 'L1_gnn_phi_w2': _L1_gnn_in['phi_w2'], 'L1_gnn_phi_b2': _L1_gnn_in['phi_b2'], 'L1_gnn_theta_w': _L1_gnn_in['theta_w'], 'L1_gnn_theta_b': _L1_gnn_in['theta_b'], 'L2_gnn_Wl': _L2_gnn_in['Wl'], 'L2_gnn_bl': _L2_gnn_in['bl'], 'L2_gnn_Wr': _L2_gnn_in['Wr'], 'L2_gnn_br': _L2_gnn_in['br'], 'L3_gnn_W': _L3_gnn_in['W'], 'L3_gnn_att_src': _L3_gnn_in['att_src'], 'L3_gnn_att_dst': _L3_gnn_in['att_dst'], 'L3_gnn_bias': _L3_gnn_in['bias']}

def reference(x, src, dst, edge_attr_128, L0_gnn_W_w, L0_gnn_W_b, L0_gnn_a_w, L0_gnn_a_b, L1_gnn_ln_gamma, L1_gnn_ln_beta, L1_gnn_phi_w1, L1_gnn_phi_b1, L1_gnn_phi_w2, L1_gnn_phi_b2, L1_gnn_theta_w, L1_gnn_theta_b, L2_gnn_Wl, L2_gnn_bl, L2_gnn_Wr, L2_gnn_br, L3_gnn_W, L3_gnn_att_src, L3_gnn_att_dst, L3_gnn_bias):
    import jax
    import jax.numpy as jnp

    def _L0_gnn_ref(x, edge_index, W_w, W_b, a_w, a_b):
        import jax, jax.numpy as jnp
        import numpy as np
        N_NODES = 6250
        N_EDGES = 100000
        DIM = 128
        h = x @ W_w + W_b
        row, col = (edge_index[0], edge_index[1])
        a_src, a_dst = (a_w[:DIM], a_w[DIM:])
        e = h[row] @ a_src + h[col] @ a_dst + a_b
        e = jax.nn.leaky_relu(e, negative_slope=0.01)
        attention = jax.nn.softmax(e, axis=0)
        msg = attention * h[col]
        out = jax.ops.segment_sum(msg, row, num_segments=N_NODES)
        return out

    def _L1_gnn_ref(node_embeddings, edge_embeddings, edge_index_list, ln_gamma, ln_beta, phi_w1, phi_b1, phi_w2, phi_b2, theta_w, theta_b):
        import jax, jax.numpy as jnp
        import numpy as np
        N = 6250
        E = 100000
        D = 128
        H = 128
        LN_EPS = 1e-05

        def _layer_norm(x, gamma, beta):
            mu = jnp.mean(x, axis=-1, keepdims=True)
            var = jnp.mean(jnp.square(x - mu), axis=-1, keepdims=True)
            return (x - mu) * jax.lax.rsqrt(var + LN_EPS) * gamma + beta
        silu = jax.nn.silu
        x = _layer_norm(node_embeddings, ln_gamma, ln_beta)
        center = edge_index_list[0]
        neigh = edge_index_list[1]
        x_c = x[center]
        x_n = x[neigh]
        s = edge_embeddings + x_c + x_n
        h = silu(s) @ phi_w1 + phi_b1
        theta_edge = silu(h) @ phi_w2 + phi_b2
        edge_msg = x_n * theta_edge
        agg = jax.ops.segment_sum(edge_msg, center, num_segments=N)
        out = silu(x + agg) @ theta_w + theta_b
        return out

    def _L2_gnn_ref(x, edge_index, Wl, bl, Wr, br):
        import jax, jax.numpy as jnp
        import numpy as np
        N = 12500
        E = 100000
        D = 128
        OUT = 128
        n = x.shape[0]
        tgt = edge_index[0]
        nbr = edge_index[1]
        agg_sum = jax.ops.segment_sum(x[nbr], tgt, num_segments=n)
        deg = jax.ops.segment_sum(jnp.ones((edge_index.shape[1],), x.dtype), tgt, num_segments=n)
        agg = agg_sum / jnp.maximum(deg, 1.0)[:, None]
        out = jax.nn.relu(x @ Wl + bl + agg @ Wr + br)
        norm = jnp.linalg.norm(out, axis=1, keepdims=True) + 1e-06
        return out / norm

    def _L3_gnn_ref(x, edge_index, W, att_src, att_dst, bias):
        import jax, jax.numpy as jnp
        import numpy as np
        N = 6250
        E = 100000
        IN = 128
        OUT = 32
        H = 4
        NEG_SLOPE = 0.2
        loop = jnp.arange(N, dtype=edge_index.dtype)
        src = jnp.concatenate([edge_index[0], loop])
        dst = jnp.concatenate([edge_index[1], loop])
        h = (x @ W.T).reshape(N, H, OUT)
        a_src = (h * att_src).sum(-1)
        a_dst = (h * att_dst).sum(-1)
        alpha = a_src[src] + a_dst[dst]
        alpha = jax.nn.leaky_relu(alpha, NEG_SLOPE)
        amax = jax.ops.segment_max(alpha, dst, num_segments=N)
        ex = jnp.exp(alpha - amax[dst])
        denom = jax.ops.segment_sum(ex, dst, num_segments=N)
        w = ex / denom[dst]
        msg = h[src] * w[:, :, None]
        out = jax.ops.segment_sum(msg, dst, num_segments=N)
        return out.reshape(N, H * OUT) + bias
    edge_index = jnp.stack([src, dst])
    h = jnp.maximum(_layernorm(x, axis=-1), 0.0)
    x = x + _L0_gnn_ref(h, edge_index, L0_gnn_W_w, L0_gnn_W_b, L0_gnn_a_w, L0_gnn_a_b)
    h = jnp.maximum(_layernorm(x, axis=-1), 0.0)
    x = x + _L1_gnn_ref(h, edge_attr_128, edge_index, L1_gnn_ln_gamma, L1_gnn_ln_beta, L1_gnn_phi_w1, L1_gnn_phi_b1, L1_gnn_phi_w2, L1_gnn_phi_b2, L1_gnn_theta_w, L1_gnn_theta_b)
    h = jnp.maximum(_layernorm(x, axis=-1), 0.0)
    x = x + _L2_gnn_ref(h, edge_index, L2_gnn_Wl, L2_gnn_bl, L2_gnn_Wr, L2_gnn_br)
    h = jnp.maximum(_layernorm(x, axis=-1), 0.0)
    x = x + _L3_gnn_ref(h, edge_index, L3_gnn_W, L3_gnn_att_src, L3_gnn_att_dst, L3_gnn_bias)
    return x

_drawn_inputs = setup_inputs


def setup_inputs(seed=0):
    import zlib

    import numpy as np

    out = dict(_drawn_inputs(seed))
    spreads = {'L1_gnn_ln_gamma': (1.0, 0.2),
     'L1_gnn_ln_beta': (0.0, 0.1),
     'L1_gnn_phi_b1': (0.0, 0.1),
     'L1_gnn_phi_b2': (0.0, 0.1),
     'L1_gnn_theta_b': (0.0, 0.351),
     'L3_gnn_bias': (0.0, 0.354)}
    factors = {'L0_gnn_W_w': 8.0,
     'L0_gnn_W_b': 8.0,
     'L0_gnn_a_w': 8.0,
     'L2_gnn_Wl': 3.646,
     'L2_gnn_bl': 8.0,
     'L2_gnn_Wr': 5.027,
     'L2_gnn_br': 8.0,
     'L3_gnn_att_src': 4.364,
     'L3_gnn_att_dst': 8.0}
    for name, (base, spread) in spreads.items():
        noise = np.random.default_rng([zlib.crc32(name.encode()), seed]).standard_normal(out[name].shape)
        drawn = base * np.exp(spread * noise) if base else spread * noise
        out[name] = jnp.asarray(drawn.astype(out[name].dtype))
    for name, factor in factors.items():
        out[name] = (out[name] * factor).astype(out[name].dtype)
    return out
```

```python
import concourse.bass as bass
from concourse import mybir
from contextlib import ExitStack

F32 = mybir.dt.float32
I32 = mybir.dt.int32
BF16 = mybir.dt.bfloat16
ALU = mybir.AluOpType
ACT = mybir.ActivationFunctionType
AX = mybir.AxisListType
ENG = mybir.EngineType

P = 128
N, E, D = 6250, 206250, 128
HEADS, HEAD_DIM = 4, 32
NB = -(-N // P)
NP = NB * P
LAST = N - (NB - 1) * P
DUMMY = NP - 1
HALF = 16
PAIRS = HALF // 2
ET = 1616
E_LAST = E - (P - 1) * ET
NPAIR = -(-((E + NB * (2 * P - 1)) // (2 * P)) // (2 * PAIRS)) * 2 * PAIRS
NT = 2 * NPAIR
NH = NT // HALF
NTX = NT + 4 * HALF
SLOTS = NT * P
PAYC = NTX
W = 132
NBLK = NB + 1
EMPTY_DST = NB * P
NEG = -1.0e30
BIG = 2.0 ** 100
LN_EPS = 1e-5
assert (P * ET - E) <= HALF * P and NH % 2 == 0
BLOCK_RANGE = "block numbers are clamped to 0..NB-1 where they are made"


_names = [0]


def fresh(kind):
    _names[0] += 1
    return f"{kind}_{_names[0]}"


class PhaseSemaphores:

    def __init__(self, nc):
        self.nc, self.taken = nc, []

    def __call__(self):
        self.taken.append(self.nc.alloc_semaphore(fresh("sem")))
        return self.taken[-1]

    def give_back(self):
        self.nc.clear_and_free_semaphores(self.taken)
        self.nc.all_engine_barrier()


class Chain:

    def __init__(self, eng, sem, start=0):
        self.eng, self.sem, self.n, self.start = eng, sem, 0, start

    def link(self, ins):
        self.n += 1
        ins.then_inc(self.sem, 1)
        self.eng.wait_ge(self.sem, self.start + self.n)


def bc(ap, shape):
    return ap.broadcast_to(shape)


def flat(ap):
    return ap.rearrange("p a b -> p (a b)")


def gnn_kernel(nc, ins, out):
    es = ExitStack()
    sb = lambda shape, dt=F32: es.enter_context(nc.sbuf_tensor(fresh("buf"), shape, dt))
    dram = lambda name, shape, dt=F32: nc.dram_tensor(name, shape, dt).ap()

    pay_a = dram("payload_by_src", (P * PAYC, 4), I32)
    pay_b = dram("payload_by_dst", (P * PAYC, 4), I32)
    listed = dram("records_as_listed", (P * ET, 4), I32)
    table = dram("node_rows", (NP, W))
    table1 = dram("node_rows_ln", (NP, D))
    kept = dram("kept_rows", (NH, P, HALF * W))

    with es:
        x_sb = sb([P, NB, D])
        iota = sb([P, P])
        ident = sb([P, P])
        ones = sb([P, P])
        idx = sb([P, NTX], I32)
        eid = sb([P, NTX], I32)
        loc = sb([P, NTX])
        blk_a = sb([1, NPAIR + 2 * PAIRS], I32)
        blk_b = sb([1, NPAIR + 2 * PAIRS], I32)

        sort_phase(nc, ins, x_sb, iota, ident, ones, pay_a, pay_b, blk_a, blk_b, listed)

        agg = sb([P, NB, W])
        tab = sb([P, NB, W])
        load_order(nc, pay_a, idx, eid, loc)
        c = dict(iota=iota, ident=ident, ones=ones, idx=idx, eid=eid, loc=loc, agg=agg, tab=tab, x=x_sb, table=table, kept=kept)

        with nc.sbuf_tensor([P, NB, 1], F32) as a_src:
            l0_nodes(nc, c, ins, a_src)
            l0_edges(nc, c, ins, blk_a, a_src)
        l0_finish(nc, c)
        l1_nodes(nc, c, ins, table1)
        l1_edges(nc, c, ins, blk_a, table1)
        l1_finish(nc, c, ins)
        l2_nodes(nc, c)
        l2_edges(nc, c, blk_a)
        l2_finish(nc, c, ins)
        load_order_by_dst(nc, pay_b, ones, blk_b, idx, loc)
        with nc.sbuf_tensor([P, NB, 2 * HEADS], F32) as seg:
            l3_nodes(nc, c, ins, seg)
            l3_max(nc, c, blk_b, seg)
            l3_self(nc, c, seg)
            l3_edges(nc, c, blk_b, seg)
        l3_finish(nc, c, ins)
        store_phase(nc, x_sb, out)


def sort_phase(nc, ins, x_sb, iota, ident, ones, pay_a, pay_b, blk_a, blk_b, listed):
    es = ExitStack()
    sb = lambda shape, dt=F32: es.enter_context(nc.sbuf_tensor(fresh("buf"), shape, dt))
    sem = PhaseSemaphores(nc)
    es.callback(sem.give_back)
    G = HALF // 2
    with es:
        src, dst, eno = sb([P, ET], I32), sb([P, ET], I32), sb([P, ET], I32)
        after = sb([P, ET], I32)
        falls, unsorted = sb([P, 1]), sb([1, 1], I32)
        gain, qstep = sb([P, NBLK]), sb([1, NPAIR + 2 * PAIRS])
        qrun, qfrom = sb([1, NPAIR + 2 * PAIRS]), sb([1, NPAIR + 2 * PAIRS], I32)
        blkf, mask, scan, pos = sb([P, ET]), sb([P, ET]), sb([P, ET]), sb([P, ET])
        addr = [sb([P, ET], I32), sb([P, ET], I32)]
        pay = [sb([P, ET, 4], I32)]
        pay.append(sb([P, ET, 4], I32))
        empty = sb([P, PAYC // 4, 4], I32)
        below, bno = sb([P, P]), sb([P, NBLK])
        cnt, off, pairs_f, cum, zero = (sb([P, NBLK]) for _ in range(5))
        pairs_i = sb([P, NBLK], I32)
        qno, qblk = sb([1, NPAIR + 2 * PAIRS]), sb([1, NPAIR + 2 * PAIRS])
        pos_st, pay_st = sb([P, 2, G], I32), sb([P, 2, G, 4], I32)
        ps = es.enter_context(nc.psum_tensor(fresh("psum"), [P, 3, 512], F32))
        loaded, made, filled, dve_chain, pool_chain, counted, prefixed, ranked = (sem() for _ in range(8))
        staged, slot_free, out0, out1 = (sem() for _ in range(4))
        rank_a, rank_b, scattering, consts = sem(), sem(), sem(), sem()
        recorded, in_dram, ran, counted_falls, fell, run_known = (sem() for _ in range(6))
        assert PAYC % 4 == 0 and ET % (2 * G) == 0

        with nc.Block() as block:
            @block.sync
            def _(sp):
                sp.wait_ge(made, 1)
                for b, e in ((src, ins["src"]), (dst, ins["dst"])):
                    sp.dma_start(b[0:P - 1, :], e[0:(P - 1) * ET].rearrange("(p t) -> p t", t=ET)).then_inc(loaded, 16)
                    sp.dma_start(b[P - 1:P, 0:E_LAST], e[(P - 1) * ET:E].rearrange("(p t) -> p t", p=1)).then_inc(loaded, 16)
                sp.dma_start(after[0:P - 1, :], ins["dst"][1:1 + (P - 1) * ET].rearrange("(p t) -> p t", t=ET)).then_inc(loaded, 16)
                sp.dma_start(after[P - 1:P, 0:E_LAST - 1], ins["dst"][1 + (P - 1) * ET:E].rearrange("(p t) -> p t", p=1)).then_inc(loaded, 16)
                sp.dma_start(x_sb[:, 0:NB - 1, :], ins["x"][0:(NB - 1) * P, :].rearrange("(b p) d -> p b d", p=P)).then_inc(loaded, 16)
                sp.dma_start(x_sb[0:LAST, NB - 1, :], ins["x"][(NB - 1) * P:N, :]).then_inc(loaded, 16)
                sp.wait_ge(made, 2)
                for o in (pay_a, pay_b):
                    v = o.rearrange("(p t) c -> p (t c)", p=P)
                    for k in range(4):
                        sp.dma_start(v[:, k * PAYC:(k + 1) * PAYC], empty[:].rearrange("p t c -> p (t c)")).then_inc(filled, 16)
                sp.wait_ge(recorded, 1)
                sp.dma_start(listed.rearrange("(p t) c -> p (t c)", t=ET), pay[1][:].rearrange("p t c -> p (t c)")).then_inc(in_dram, 16)
                sp.wait_ge(in_dram, 16)
                sp.wait_ge(filled, 8 * 16)
                sp.wait_ge(run_known, 1)
                slots = pay_b.rearrange("(p t) c -> p t c", p=P)
                scattered = sp.value_load(unsorted[0:1, 0:1], min_val=0, max_val=1)
                with sp.If(1 - scattered):
                    with sp.Fori(0, NPAIR // PAIRS) as i:
                        starts = nc.values_load_multi_w_load_instructions(
                            qfrom[0:1, bass.ds(i * PAIRS, PAIRS)], engines=[ENG.SP], min_val=0, max_val=E,
                            skip_runtime_bounds_check_because="the starts are clamped to 0..E where they are made")[1]
                        for q in range(PAIRS):
                            sp.dma_start(slots[:, bass.ds(i * (2 * PAIRS) + 2 * q, 2), :],
                                         listed[bass.ds(starts[q], 2 * P), :].rearrange("(p s) c -> p s c", s=2)).then_inc(ran, 16)
                    sp.wait_ge(ran, 16 * NPAIR)

            @block.gpsimd
            def _(pool):
                ch = Chain(pool, pool_chain)
                nc.gpsimd.iota(eno[:], [[1, ET]], base=0, channel_multiplier=ET)
                nc.gpsimd.iota(iota[:], [[1, P]], base=0, channel_multiplier=0, allow_small_or_imprecise_dtypes=True)
                nc.gpsimd.iota(bno[:], [[1, NBLK]], base=0, channel_multiplier=0, allow_small_or_imprecise_dtypes=True)
                nc.gpsimd.iota(qno[:], [[1, NPAIR + 2 * PAIRS]], base=0, channel_multiplier=0, allow_small_or_imprecise_dtypes=True)
                nc.gpsimd.memset(ones[:], 1.0)
                ch.link(nc.gpsimd.memset(ident[:], 0.0))
                ch.link(nc.gpsimd.affine_select(out=ident[:], in_=ident[:], compare_op=ALU.not_equal, fill=1.0, base=0,
                                                pattern=[[-1, P]], channel_multiplier=1))
                ch.link(nc.gpsimd.memset(below[:], 0.0))
                ch.link(nc.gpsimd.affine_select(out=below[:], in_=below[:], compare_op=ALU.is_ge, fill=1.0, base=0,
                                                pattern=[[-1, P]], channel_multiplier=1))
                pool.sem_inc(consts, 1)
                pool.wait_ge(filled, 8 * 16)
                def scatter(k):
                    with pool.Fori(0, ET // (2 * G)) as i:
                        for h in range(2):
                            pool.wait_ge(staged, 2 * i + (h + 1 + k * (ET // G)))
                            pool.sem_inc(scattering, 1)
                            for t in range(G):
                                nc.gpsimd.indirect_dma_start(
                                    (pay_a, pay_b)[k], bass.IndirectOffsetOnAxis(ap=pos_st[:, h, t:t + 1], axis=0),
                                    pay_st[:, h, t, :], None).then_inc((out0, out1)[h], 16)
                    pool.wait_ge(out0, (k + 1) * 16 * ET // 2)
                    pool.wait_ge(out1, (k + 1) * 16 * ET // 2)

                scatter(0)
                pool.wait_ge(run_known, 1)
                with pool.If(pool.value_load(unsorted[0:1, 0:1], min_val=0, max_val=1)):
                    scatter(1)

            @block.scalar
            def _(act):
                n = ET // (2 * G)

                def stage(k):
                    for h in range(2):
                        if k:
                            act.wait_ge((out0, out1)[h], 16 * G * n)
                        nc.scalar.copy(pos_st[:, h, :], addr[k][:, h * G:(h + 1) * G])
                        nc.scalar.copy(pay_st[:, h], pay[k][:, h * G:(h + 1) * G, :]).then_inc(staged, 1)
                    with act.Fori(1, n) as i:
                        for h in range(2):
                            act.wait_ge((out0, out1)[h], 16 * G * i + 16 * G * n * k)
                            nc.scalar.copy(pos_st[:, h, :], addr[k][:, bass.ds(i * (2 * G) + h * G, G)])
                            nc.scalar.copy(pay_st[:, h], pay[k][:, bass.ds(i * (2 * G) + h * G, G), :]).then_inc(staged, 1)

                act.wait_ge(rank_a, 1)
                stage(0)
                act.wait_ge(rank_b, 1)
                act.wait_ge(run_known, 1)
                with act.If(act.value_load(unsorted[0:1, 0:1], min_val=0, max_val=1)):
                    stage(1)

            @block.tensor
            def _(pe):
                for k in range(2):
                    pe.wait_ge(counted, k + 1)
                    if k == 0:
                        pe.wait_ge(consts, 1)
                    nc.tensor.matmul(ps[:, 0, 0:NBLK], below[:], cnt[:], start=True, stop=True)
                    nc.tensor.matmul(ps[:, 1, 0:NBLK], ones[:], cnt[:], start=True, stop=True).then_inc(prefixed, 1)
                pe.wait_ge(counted_falls, 1)
                nc.tensor.matmul(ps[:, 2, 0:1], ones[:], falls[:], start=True, stop=True).then_inc(fell, 1)

            @block.vector
            def _(dve):
                ch = Chain(dve, dve_chain)
                ch.link(nc.vector.memset(x_sb[:, NB - 1, :], 0.0))
                ch.link(nc.vector.memset(src[:], EMPTY_DST))
                ch.link(nc.vector.memset(dst[:], EMPTY_DST))
                ch.link(nc.vector.memset(after[:], EMPTY_DST))
                dve.sem_inc(made, 1)
                nc.vector.memset(empty[:, :, 0:1], DUMMY)
                nc.vector.memset(empty[:, :, 1:2], 0)
                nc.vector.memset(empty[:, :, 2:3], -1)
                ch.link(nc.vector.memset(empty[:, :, 3:4], EMPTY_DST))
                dve.sem_inc(made, 1)
                ch.link(nc.vector.memset(zero[:], 0.0))
                dve.wait_ge(consts, 1)
                dve.wait_ge(loaded, 128)
                n = ch.n

                def pairs_of_blocks(k, n):
                    ch = Chain(dve, dve_chain, start=n)
                    ch.link(nc.vector.memset(qblk[:], 0.0))
                    n += ch.n
                    with dve.Fori(0, NB) as b:
                        lp = Chain(dve, dve_chain, start=b + n)
                        lp.link(nc.vector.scalar_tensor_tensor(qblk[:], qno[:], cum[0:1, bass.ds(b, 1)], qblk[:], ALU.is_ge, ALU.add))
                    n += NB
                    ch = Chain(dve, dve_chain, start=n)
                    ch.link(nc.vector.tensor_scalar((blk_a, blk_b)[k][:], qblk[:], float(NB - 1), None, ALU.min))
                    return n + ch.n

                def runs_of_list(n):
                    ch = Chain(dve, dve_chain, start=n)
                    ch.link(nc.vector.tensor_scalar(qrun[:], qno[:], float(2 * P), None, ALU.mult))
                    n += ch.n
                    with dve.Fori(0, NB) as b:
                        lp = Chain(dve, dve_chain, start=b * 2 + n)
                        lp.link(nc.vector.tensor_scalar(qstep[:], qno[:], cum[0:1, bass.ds(b, 1)], gain[0:1, bass.ds(b, 1)], ALU.is_ge, ALU.mult))
                        lp.link(nc.vector.tensor_tensor(qrun[:], qrun[:], qstep[:], ALU.add))
                    n += NB * 2
                    ch = Chain(dve, dve_chain, start=n)
                    ch.link(nc.vector.tensor_scalar(qfrom[:], qrun[:], float(E), None, ALU.min))
                    ch.link(nc.vector.tensor_tensor(mask[:], dst[:], after[:], ALU.is_gt))
                    nc.vector.tensor_reduce(falls[:], mask[:], AX.X, ALU.add).then_inc(counted_falls, 1)
                    dve.wait_ge(fell, 1)
                    ch.link(nc.vector.tensor_scalar(unsorted[:], ps[0:1, 2, 0:1], 1.0, None, ALU.min))
                    dve.sem_inc(run_known, 1)
                    return n + ch.n

                for k, (key, other) in enumerate(((src, dst), (dst, src))):
                    ch = Chain(dve, dve_chain, start=n)
                    ch.link(nc.vector.tensor_scalar(addr[k][:], key[:], 7, None, ALU.logical_shift_right))
                    ch.link(nc.vector.tensor_copy(blkf[:], addr[k][:]))
                    ch.link(nc.vector.tensor_scalar(addr[k][:], key[:], P - 1, None, ALU.bitwise_and))
                    nc.vector.tensor_copy(pay[k][:, :, 0:1], other[:].unsqueeze(2))
                    nc.vector.tensor_copy(pay[k][:, :, 1:2], eno[:].unsqueeze(2))
                    nc.vector.tensor_copy(pay[k][:, :, 2:3], addr[k][:].unsqueeze(2))
                    ch.link(nc.vector.tensor_copy(pay[k][:, :, 3:4], key[:].unsqueeze(2)))
                    n += ch.n
                    if k:
                        dve.sem_inc(recorded, 1)
                    with dve.Fori(0, NBLK) as b:
                        lp = Chain(dve, dve_chain, start=b * 2 + n)
                        lp.link(nc.vector.tensor_scalar(mask[:], blkf[:], bno[:, bass.ds(b, 1)], None, ALU.is_equal))
                        lp.link(nc.vector.tensor_reduce(cnt[:, bass.ds(b, 1)], mask[:], AX.X, ALU.add))
                    n += NBLK * 2
                    dve.sem_inc(counted, 1)
                    dve.wait_ge(prefixed, k + 1)
                    ch = Chain(dve, dve_chain, start=n)
                    ch.link(nc.vector.tensor_scalar(pairs_i[:], ps[:, 1, 0:NBLK], float(2 * P - 1), None, ALU.add))
                    ch.link(nc.vector.tensor_scalar(pairs_i[:], pairs_i[:], 8, None, ALU.logical_shift_right))
                    ch.link(nc.vector.tensor_copy(pairs_f[:], pairs_i[:]))
                    ch.link(nc.vector.tensor_tensor_scan(cum[:], pairs_f[:], zero[:], 0.0, ALU.add, ALU.add))
                    ch.link(nc.vector.scalar_tensor_tensor(gain[:], pairs_f[:], float(-2 * P), ps[:, 1, 0:NBLK], ALU.mult, ALU.add))
                    ch.link(nc.vector.tensor_tensor(pairs_f[:], cum[:], pairs_f[:], ALU.subtract))
                    ch.link(nc.vector.memset(pairs_f[:, NB:NBLK], float(NPAIR)))
                    ch.link(nc.vector.scalar_tensor_tensor(off[:], pairs_f[:], float(2 * P), ps[:, 0, 0:NBLK], ALU.mult, ALU.add))
                    n += ch.n
                    if k:
                        n = pairs_of_blocks(k, n)
                        n = runs_of_list(n)
                    ch = Chain(dve, dve_chain, start=n)
                    ch.link(nc.vector.memset(pos[:], 0.0))
                    n += ch.n
                    with dve.Fori(0, NBLK) as b:
                        lp = Chain(dve, dve_chain, start=b * 4 + n)
                        lp.link(nc.vector.tensor_scalar(mask[:], blkf[:], bno[:, bass.ds(b, 1)], None, ALU.is_equal))
                        lp.link(nc.vector.tensor_tensor_scan(scan[:], mask[:], mask[:], off[:, bass.ds(b, 1)], ALU.add, ALU.max))
                        lp.link(nc.vector.tensor_tensor(scan[:], scan[:], mask[:], ALU.mult))
                        lp.link(nc.vector.tensor_tensor(pos[:], pos[:], scan[:], ALU.add))
                    n += NBLK * 4
                    ch = Chain(dve, dve_chain, start=n)
                    si, lo = addr[k], scan[:].bitcast(I32)
                    ch.link(nc.vector.tensor_scalar(si[:], pos[:], -1.0, None, ALU.add))
                    ch.link(nc.vector.tensor_scalar(lo, si[:], P - 1, None, ALU.bitwise_and))
                    ch.link(nc.vector.tensor_scalar(si[:], si[:], 7, None, ALU.logical_shift_right))
                    ch.link(nc.vector.scalar_tensor_tensor(mask[:], lo, float(PAYC), si[:], ALU.mult, ALU.add))
                    ch.link(nc.vector.tensor_copy(si[:], mask[:]))
                    n += ch.n
                    dve.sem_inc((rank_a, rank_b)[k], 1)
                    if not k:
                        n = pairs_of_blocks(k, n)


def load_order(nc, pay, idx, eid, loc):
    with (nc.sbuf_tensor([P, NTX, 4], I32) as rec, nc.semaphore() as loaded, nc.semaphore() as spread, nc.Block() as block):
        @block.sync
        def _(sp):
            sp.dma_start(rec[:].rearrange("p t c -> p (t c)"), pay.rearrange("(p t) c -> p (t c)", p=P)).then_inc(loaded, 16)

        @block.vector
        def _(dve):
            dve.wait_ge(loaded, 16)
            nc.vector.tensor_copy(idx[:].unsqueeze(2), rec[:, :, 0:1])
            nc.vector.tensor_copy(eid[:].unsqueeze(2), rec[:, :, 1:2])
            nc.vector.tensor_copy(loc[:].unsqueeze(2), rec[:, :, 2:3]).then_inc(spread, 1)
            dve.wait_ge(spread, 1)
            nc.vector.memset(idx[:, NT:NTX], DUMMY)
            nc.vector.memset(eid[:, NT:NTX], 0)
            nc.vector.memset(loc[:, NT:NTX], -1.0).then_inc(spread, 1)
            dve.wait_ge(spread, 2)


def load_order_by_dst(nc, pay, ones, blk, idx, loc):
    es = ExitStack()
    sb = lambda shape, dt=F32: es.enter_context(nc.sbuf_tensor(fresh("buf"), shape, dt))
    sem = lambda: es.enter_context(nc.semaphore(fresh("sem")))
    HP = NPAIR // 2
    assert HP <= 512
    with es:
        rec, blkf, place, valid, node = sb([P, NTX, 4], I32), sb([1, NPAIR]), sb([P, NT]), sb([P, NT]), sb([P, NT])
        ps = es.enter_context(nc.psum_tensor(fresh("psum"), [P, 2, 512], F32))
        loaded, floated, spread, dve_chain = (sem() for _ in range(4))
        with nc.Block() as block:
            @block.sync
            def _(sp):
                sp.dma_start(rec[:].rearrange("p t c -> p (t c)"), pay.rearrange("(p t) c -> p (t c)", p=P)).then_inc(loaded, 16)

            @block.tensor
            def _(pe):
                pe.wait_ge(floated, 1)
                for k in range(2):
                    last = nc.tensor.matmul(ps[:, k, 0:HP], ones[0:1, :], blkf[:, k * HP:(k + 1) * HP], start=True, stop=True)
                last.then_inc(spread, 1)

            @block.vector
            def _(dve):
                ch = Chain(dve, dve_chain)
                nc.vector.tensor_copy(blkf[:], blk[:, 0:NPAIR]).then_inc(floated, 1)
                dve.wait_ge(loaded, 16)
                ch.link(nc.vector.tensor_copy(place[:].unsqueeze(2), rec[:, 0:NT, 3:4]))
                dve.wait_ge(spread, 1)
                for k in range(2):
                    part = place[:, k * 2 * HP:(k + 1) * 2 * HP].rearrange("p (q s) -> p q s", s=2)
                    ch.link(nc.vector.scalar_tensor_tensor(part, bc(ps[:, k, 0:HP].unsqueeze(2), [P, HP, 2]), float(-P), part, ALU.mult, ALU.add))
                ch.link(nc.vector.tensor_scalar(valid[:], place[:], 0.0, None, ALU.is_ge))
                ch.link(nc.vector.scalar_tensor_tensor(valid[:], place[:], float(P), valid[:], ALU.is_lt, ALU.mult))
                ch.link(nc.vector.scalar_tensor_tensor(place[:], place[:], 1.0, valid[:], ALU.add, ALU.mult))
                ch.link(nc.vector.tensor_scalar(loc[:, 0:NT], place[:], -1.0, None, ALU.add))
                ch.link(nc.vector.tensor_copy(node[:].unsqueeze(2), rec[:, 0:NT, 0:1]))
                ch.link(nc.vector.scalar_tensor_tensor(node[:], node[:], float(-DUMMY), valid[:], ALU.add, ALU.mult))
                ch.link(nc.vector.tensor_scalar(idx[:, 0:NT], node[:], float(DUMMY), None, ALU.add))
                nc.vector.memset(idx[:, NT:NTX], DUMMY)
                ch.link(nc.vector.memset(loc[:, NT:NTX], -1.0))


KB = 7
assert NB % KB == 0


def ln_stats(ch, act, src, tmp, st):
    sh = [P, NB, D]
    ch.link(nc_v(ch).tensor_reduce(st["mean"][:], src, AX.X, ALU.add))
    ch.link(nc_v(ch).tensor_scalar(st["mean"][:], st["mean"][:], 1.0 / D, None, ALU.mult))
    ch.link(nc_v(ch).tensor_tensor(tmp[:], src, bc(st["mean"][:].unsqueeze(2), sh), ALU.subtract))
    ch.link(nc_v(ch).tensor_tensor(tmp[:], tmp[:], tmp[:], ALU.mult))
    ch.link(nc_v(ch).tensor_reduce(st["var"][:], tmp[:], AX.X, ALU.add))
    nc_v(ch).tensor_scalar(st["var"][:], st["var"][:], 1.0 / D, LN_EPS, ALU.mult, ALU.add).then_inc(st["var_ready"], 1)
    st["n"] += 1
    ch.eng.wait_ge(st["sd_ready"], st["n"])
    ch.link(nc_v(ch).reciprocal(st["rstd"][:], st["sd"][:]))
    ch.link(nc_v(ch).scalar_tensor_tensor(st["nmr"][:], st["mean"][:], -1.0, st["rstd"][:], ALU.mult, ALU.mult))


def nc_v(ch):
    return ch.eng.bass.vector


def ln_sqrt(nc, act, st, n):
    act.wait_ge(st["var_ready"], n)
    nc.scalar.activation(st["sd"][:], st["var"][:], ACT.Sqrt).then_inc(st["sd_ready"], 1)


def ln_buffers(sb, sem):
    return dict(mean=sb([P, NB]), var=sb([P, NB]), sd=sb([P, NB]), rstd=sb([P, NB]), nmr=sb([P, NB]),
                var_ready=sem(), sd_ready=sem(), n=0)


def mm_buffers(es, nc, sb, sem, j):
    return dict(stage=sb([P, KB, j, P]), hT=sb([P, j, P]), psT=es.enter_context(nc.psum_tensor(fresh("psum"), [P, j, 512], F32)),
                psO=es.enter_context(nc.psum_tensor(fresh("psum"), [P, 512], F32)), staged=sem(), transposed=sem(), turned=sem(),
                produced=sem(), consumed=sem(), j=j)


def mm_scalar(act, m, fill):
    with act.Fori(0, NB // KB) as i:
        for k in range(KB):
            act.wait_ge(m["transposed"], i * KB + (k + 1))
            fill(k, i * KB + k, m["stage"][:, k]).then_inc(m["staged"], 1)


def mm_tensor(nc, pe, m, ident, weights):
    pe.sem_inc(m["transposed"], KB)
    with pe.Fori(0, NB // KB) as i:
        for k in range(KB):
            pe.wait_ge(m["staged"], i * KB + (k + 1))
            for j in range(m["j"]):
                t = nc.tensor.transpose(m["psT"][:, j, 0:P], m["stage"][:, k, j, :], ident[:])
            t.then_inc(m["transposed"], 1)
            pe.wait_ge(m["turned"], i * KB + (k + 1))
            for j in range(m["j"]):
                t = nc.tensor.matmul(m["psO"][:, 0:D], m["hT"][:, j, :], weights[j], start=(j == 0), stop=(j == m["j"] - 1))
            t.then_inc(m["produced"], 1)


def mm_vector(nc, dve, m, use):
    with dve.Fori(0, NB // KB) as i:
        for k in range(KB):
            dve.wait_ge(m["transposed"], i * KB + (k + 1 + KB))
            nc.vector.tensor_copy(m["hT"][:], m["psT"][:, :, 0:P]).then_inc(m["turned"], 1)
            dve.wait_ge(m["produced"], i * KB + (k + 1))
            use(i * KB + k, m["psO"][:, 0:D], i, k)


def row_of(v):
    return v.rearrange("(o d) -> o d", o=1)


def l0_nodes(nc, c, ins, a_src):
    es = ExitStack()
    sb = lambda shape, dt=F32: es.enter_context(nc.sbuf_tensor(fresh("buf"), shape, dt))
    sem = lambda: es.enter_context(nc.semaphore(fresh("sem")))
    tab = c["tab"]
    with es:
        tmp, st, m = sb([P, NB, D]), ln_buffers(sb, sem), mm_buffers(es, nc, sb, sem, 1)
        w, wb, aw = sb([D, D]), sb([P, D]), sb([P, 2, D])
        loaded, stats, dve_chain, tabled, stored, scored = (sem() for _ in range(6))
        with nc.Block() as block:
            @block.sync
            def _(sp):
                sp.dma_start(w[:], ins["L0_gnn_W_w"]).then_inc(loaded, 16)
                sp.dma_start(wb[:], row_of(ins["L0_gnn_W_b"]).broadcast_to([P, D])).then_inc(loaded, 16)
                for k in range(2):
                    sp.dma_start(aw[:, k], ins["L0_gnn_a_w"][k * D:(k + 1) * D, :].rearrange("d o -> o d").broadcast_to([P, D])).then_inc(loaded, 16)
                sp.wait_ge(tabled, 1)
                sp.dma_start(c["table"].rearrange("(b p) w -> p b w", p=P), tab[:]).then_inc(stored, 16)
                sp.wait_ge(stored, 16)

            @block.scalar
            def _(act):
                ln_sqrt(nc, act, st, 1)
                act.wait_ge(stats, 1)
                mm_scalar(act, m, lambda k, b, stage: nc.scalar.activation(
                    stage[:, 0, :], flat(c["x"][:, bass.ds(b, 1), :]), ACT.Relu,
                    bias=st["nmr"][:, bass.ds(b, 1)], scale=st["rstd"][:, bass.ds(b, 1)]))

            @block.tensor
            def _(pe):
                pe.wait_ge(loaded, 64)
                mm_tensor(nc, pe, m, c["ident"], [w[:]])

            @block.vector
            def _(dve):
                ch = Chain(dve, dve_chain)
                ln_stats(ch, None, c["x"][:], tmp, st)
                dve.sem_inc(stats, 1)
                ch.link(nc.vector.memset(tab[:], 0.0))
                dve.wait_ge(loaded, 64)
                mm_vector(nc, dve, m, lambda b, ps, i, k: nc.vector.tensor_tensor(
                    flat(tab[:, bass.ds(b, 1), 0:D]), ps, wb[:], ALU.add).then_inc(m["consumed"], 1))
                dve.wait_ge(m["consumed"], NB)
                nc.vector.memset(tab[:, :, D:D + 1], 1.0)
                ch.link(nc.vector.tensor_tensor(tmp[:], tab[:, :, 0:D], bc(aw[:, 0:1], [P, NB, D]), ALU.mult))
                ch.link(nc.vector.tensor_reduce(a_src[:], tmp[:], AX.X, ALU.add))
                ch.link(nc.vector.tensor_tensor(tmp[:], tab[:, :, 0:D], bc(aw[:, 1:2], [P, NB, D]), ALU.mult))
                ch.link(nc.vector.tensor_reduce(tab[:, :, D + 1:D + 2], tmp[:], AX.X, ALU.add))
                dve.sem_inc(tabled, 1)


def half_of(i, h, ahead=0):
    return i * (2 * HALF) + (h + ahead) * HALF


def onehot(nc, c, oh, tile0):
    return nc.vector.tensor_tensor(oh, bc(c["iota"][:].unsqueeze(1), [P, HALF, P]),
                                   bc(c["loc"][:, bass.ds(tile0, HALF)].unsqueeze(2), [P, HALF, P]), ALU.is_equal)


def gather_half(nc, pool, table, stage, rows, sem, used):
    for t in range(HALF):
        nc.gpsimd.indirect_dma_start(rows[:, t, 0:used], None, table, bass.IndirectOffsetOnAxis(ap=stage[:, t:t + 1], axis=0)).then_inc(sem, 16)


def pair_blocks(nc, engine, blk, i, h, ahead=0):
    return nc.values_load_multi_w_load_instructions(
        blk[0:1, bass.ds(i * (2 * PAIRS) + (h + ahead) * PAIRS, PAIRS)], engines=[engine], min_val=0, max_val=NB - 1,
        skip_runtime_bounds_check_because=BLOCK_RANGE)[1]


def sum_pairs(nc, ps, oh, rows, width):
    for q in range(PAIRS):
        for s in range(2):
            last = nc.tensor.matmul(ps[:, q // 3, (q % 3) * W:(q % 3) * W + width], oh[:, 2 * q + s, :], rows[:, 2 * q + s, 0:width],
                                    start=(s == 0), stop=(s == 1))
    return last


def add_pairs(nc, dve, agg, ps, blocks, width, added, i, h):
    for q in range(PAIRS):
        dve.wait_ge(added, i * (2 * PAIRS) + (h * PAIRS + q + 1))
        a = flat(agg[:, bass.ds(blocks[q], 1), 0:width])
        nc.vector.tensor_tensor(a, a, ps[:, q // 3, (q % 3) * W:(q % 3) * W + width], ALU.add).then_inc(added, 1)


def turn_onehot(nc, c, oh, psT, sg):
    for t in range(4):
        last = nc.tensor.transpose(psT[:, sg % 2, t * P:(t + 1) * P], oh[:, 4 * sg + t, :], c["ident"][:])
    return last


def l0_edges(nc, c, ins, blk, a_src):
    es = ExitStack()
    sb = lambda shape, dt=F32: es.enter_context(nc.sbuf_tensor(fresh("buf"), shape, dt))
    sem = PhaseSemaphores(nc)
    es.callback(sem.give_back)
    agg = c["agg"]
    with es:
        stage, rows, oh = sb([P, 2, HALF], I32), sb([P, 2, HALF, W]), sb([P, 2, HALF, P])
        hot16, ohT = sb([P, 2, HALF, P]), sb([P, 2, 4 * P])
        ab, e1, e2, pen, p = sb([P, 1]), sb([P, HALF]), sb([P, HALF]), sb([P, HALF]), sb([P, 2, HALF])
        mx, m1, mrun, mold, negm, fac = sb([P, 1]), sb([1, 1]), sb([1, 1]), sb([P, 1]), sb([P, 1]), sb([P, 2])
        psT = es.enter_context(nc.psum_tensor(fresh("psum"), [P, 2, 512], F32))
        psE = es.enter_context(nc.psum_tensor(fresh("psum"), [P, 512], F32))
        psM = es.enter_context(nc.psum_tensor(fresh("psum"), [P, 2, 512], F32))
        psA = es.enter_context(nc.psum_tensor(fresh("psum"), [P, 3, 512], F32))
        (loaded, staged, got0, got1, gathering, hot, ohT_ps, ohT_ready, expanded, maxed, max_turned, max_run, max_spread, newmax,
         weights, weighted, summed, scaled, added, dve_chain) = (sem() for _ in range(20))
        got = (got0, got1)
        DV = 6
        with nc.Block() as block:
            @block.sync
            def _(sp):
                sp.dma_start(ab[:], row_of(ins["L0_gnn_a_b"]).broadcast_to([P, 1])).then_inc(loaded, 16)
                sp.wait_ge(loaded, 16)

            @block.gpsimd
            def _(pool):
                def fetch(n, h):
                    pool.wait_ge(staged, n)
                    pool.sem_inc(gathering, 1)
                    gather_half(nc, pool, c["table"], stage[:, h], rows[:, h], got[h], W)
                fetch(1, 0)
                with pool.Fori(0, NH // 2) as i:
                    for h in range(2):
                        fetch(2 * i + (h + 2), 1 - h)

            @block.scalar
            def _(act):
                def copies(n):
                    for sg in range(4):
                        act.wait_ge(ohT_ps, 4 * n + (sg + 1))
                        if sg >= 2:
                            act.wait_ge(expanded, 4 * n + (sg - 1))
                        nc.scalar.copy(ohT[:, sg % 2, :], psT[:, sg % 2, :]).then_inc(ohT_ready, 1)

                def weigh(n, h):
                    act.wait_ge(newmax, n + 1)
                    nc.scalar.activation(p[:, h, :], e2[:], ACT.Exp, bias=negm[:])
                    nc.scalar.activation(fac[:, h:h + 1], mold[:], ACT.Exp, bias=negm[:]).then_inc(weights, 1)

                nc.scalar.copy(stage[:, 0, :], c["idx"][:, 0:HALF]).then_inc(staged, 1)
                nc.scalar.copy(stage[:, 1, :], c["idx"][:, HALF:2 * HALF]).then_inc(staged, 1)
                copies(0)
                weigh(0, 0)
                with act.Fori(0, NH // 2) as i:
                    for h in range(2):
                        copies(2 * i + (h + 1))
                        act.wait_ge(added, i * (2 * PAIRS) + (h * PAIRS + 1))
                        act.wait_ge(weights, 2 * i + (h + 1))
                        nc.scalar.activation(flat(agg[:]), flat(agg[:]), ACT.Copy, scale=fac[:, h:h + 1]).then_inc(scaled, 1)
                        act.wait_ge(summed, 2 * i + (h + 1))
                        nc.scalar.copy(stage[:, h, :], c["idx"][:, bass.ds(half_of(i, h, 2), HALF)]).then_inc(staged, 1)
                        weigh(2 * i + (h + 1), 1 - h)

            @block.tensor
            def _(pe):
                def spread(n, h, blocks):
                    pe.wait_ge(hot, n + 1)
                    for sg in range(4):
                        if sg >= 2:
                            pe.wait_ge(ohT_ready, 4 * n + (sg - 1))
                        turn_onehot(nc, c, hot16[:, h], psT, sg).then_inc(ohT_ps, 1)
                        if sg >= 1:
                            expand(n, sg - 1, blocks)
                    expand(n, 3, blocks)

                def maximum(n):
                    pe.wait_ge(maxed, n + 1)
                    nc.tensor.transpose(psM[0:1, 0, 0:P], mx[:], c["ident"][:]).then_inc(max_turned, 1)
                    pe.wait_ge(max_run, n + 1)
                    nc.tensor.matmul(psM[:, 1, 0:1], c["ones"][0:1, :], mrun[:], start=True, stop=True).then_inc(max_spread, 1)

                def expand(n, sg, blocks):
                    pe.wait_ge(ohT_ready, 4 * n + (sg + 1))
                    for t in range(4):
                        last = nc.tensor.matmul(psE[:, 4 * sg + t:4 * sg + t + 1], ohT[:, sg % 2, t * P:(t + 1) * P],
                                                flat(a_src[:, bass.ds(blocks[(4 * sg + t) // 2], 1), :]), start=True, stop=True)
                    last.then_inc(expanded, 1)

                b0 = nc.values_load_multi_w_load_instructions(blk[0:1, 0:PAIRS], engines=[ENG.PE], min_val=0, max_val=NB - 1,
                                                              skip_runtime_bounds_check_because=BLOCK_RANGE)[1]
                spread(0, 0, b0)
                maximum(0)
                with pe.Fori(0, NH // 2) as i:
                    for h in range(2):
                        blocks = pair_blocks(nc, ENG.PE, blk, i, h, 1)
                        spread(2 * i + (h + 1), 1 - h, blocks)
                        pe.wait_ge(weighted, 2 * i + (h + 1))
                        pe.wait_ge(got[h], 256 * i + 256)
                        pe.wait_ge(added, i * (2 * PAIRS) + (h * PAIRS + 1))
                        sum_pairs(nc, psA, oh[:, h], rows[:, h], D + 1).then_inc(summed, 1)
                        maximum(2 * i + (h + 1))

            @block.vector
            def _(dve):
                def scores(n, h, rows_at):
                    lp = Chain(dve, dve_chain, start=n * DV + 1)
                    dve.wait_ge(expanded, 4 * n + 4)
                    dve.wait_ge(got[h], rows_at)
                    ad = rows[:, h, :, D + 1:D + 2].rearrange("p t o -> p (t o)")
                    lp.link(nc.vector.scalar_tensor_tensor(e1[:], psE[:, 0:HALF], ab[:], ad, ALU.add, ALU.add))
                    lp.link(nc.vector.scalar_tensor_tensor(e2[:], e1[:], 0.01, e1[:], ALU.mult, ALU.max))
                    lp.link(nc.vector.tensor_scalar(pen[:], c["loc"][:, bass.ds(n * HALF, HALF)], 0.0, -NEG, ALU.min, ALU.mult))
                    lp.link(nc.vector.tensor_tensor(e2[:], e2[:], pen[:], ALU.add))
                    nc.vector.tensor_reduce(mx[:], e2[:], AX.X, ALU.max).then_inc(maxed, 1)

                def weigh(n, h):
                    lp = Chain(dve, dve_chain, start=n * DV + 5)
                    dve.wait_ge(max_turned, n + 1)
                    lp.link(nc.vector.tensor_reduce(m1[:], psM[0:1, 0, 0:P], AX.X, ALU.max))
                    nc.vector.tensor_tensor(mrun[:], mrun[:], m1[:], ALU.max).then_inc(max_run, 1)
                    dve.wait_ge(max_spread, n + 1)
                    lp.link(nc.vector.tensor_scalar(mold[:], negm[:], -1.0, None, ALU.mult))
                    nc.vector.tensor_scalar(negm[:], psM[:, 1, 0:1], -1.0, None, ALU.mult).then_inc(newmax, 1)
                    dve.wait_ge(weights, n + 1)
                    nc.vector.tensor_tensor(oh[:, h], hot16[:, h], bc(p[:, h, :].unsqueeze(2), [P, HALF, P]), ALU.mult).then_inc(weighted, 1)
                    assert lp.n == DV - 4

                nc.vector.memset(mrun[:], NEG)
                nc.vector.memset(negm[:], -NEG).then_inc(dve_chain, 1)
                nc.vector.memset(agg[:], 0.0).then_inc(added, 1)
                dve.wait_ge(loaded, 16)
                dve.wait_ge(dve_chain, 1)
                onehot(nc, c, hot16[:, 0], 0).then_inc(hot, 1)
                onehot(nc, c, hot16[:, 1], HALF).then_inc(hot, 1)
                scores(0, 0, 256)
                weigh(0, 0)
                with dve.Fori(0, NH // 2) as i:
                    for h in range(2):
                        scores(2 * i + (h + 1), 1 - h, 256 * i + 256 + 256 * h)
                        onehot(nc, c, hot16[:, h], half_of(i, h, 2)).then_inc(hot, 1)
                        blocks = pair_blocks(nc, ENG.DVE, blk, i, h)
                        weigh(2 * i + (h + 1), 1 - h)
                        dve.wait_ge(summed, 2 * i + (h + 1))
                        dve.wait_ge(scaled, 2 * i + (h + 1))
                        add_pairs(nc, dve, agg, psA, blocks, D + 1, added, i, h)


def l0_finish(nc, c):
    agg, x = c["agg"], c["x"]
    es = ExitStack()
    sb = lambda shape, dt=F32: es.enter_context(nc.sbuf_tensor(fresh("buf"), shape, dt))
    sem = lambda: es.enter_context(nc.semaphore(fresh("sem")))
    with es:
        z, zi = sb([P, 1]), sb([P, 1])
        ps = es.enter_context(nc.psum_tensor(fresh("psum"), [P, 512], F32))
        dve_chain, zed, total = sem(), sem(), sem()
        with nc.Block() as block:
            @block.tensor
            def _(pe):
                pe.wait_ge(zed, 1)
                nc.tensor.matmul(ps[:, 0:1], c["ones"][:], z[:], start=True, stop=True).then_inc(total, 1)

            @block.vector
            def _(dve):
                ch = Chain(dve, dve_chain)
                nc.vector.tensor_reduce(z[:], agg[:, :, D:D + 1], AX.XY, ALU.add).then_inc(zed, 1)
                dve.wait_ge(total, 1)
                ch.link(nc.vector.reciprocal(zi[:], ps[:, 0:1]))
                ch.link(nc.vector.scalar_tensor_tensor(x[:], agg[:, :, 0:D], zi[:], x[:], ALU.mult, ALU.add))


def store_phase(nc, x_sb, out):
    with nc.semaphore() as stored, nc.Block() as block:
        @block.sync
        def _(sp):
            sp.dma_start(out[0:(NB - 1) * P, :].rearrange("(b p) d -> p b d", p=P), x_sb[:, 0:NB - 1, :]).then_inc(stored, 16)
            sp.dma_start(out[(NB - 1) * P:N, :], x_sb[0:LAST, NB - 1, :]).then_inc(stored, 16)
            sp.wait_ge(stored, 32)


def norm_nodes(ch, nc, st, src, dst):
    sh = [P, NB, D]
    ch.link(nc.vector.tensor_tensor(dst, src, bc(st["rstd"][:].unsqueeze(2), sh), ALU.mult))
    ch.link(nc.vector.tensor_tensor(dst, dst, bc(st["nmr"][:].unsqueeze(2), sh), ALU.add))


def l1_nodes(nc, c, ins, table1):
    es = ExitStack()
    sb = lambda shape, dt=F32: es.enter_context(nc.sbuf_tensor(fresh("buf"), shape, dt))
    sem = lambda: es.enter_context(nc.semaphore(fresh("sem")))
    f = c["tab"][:, :, 0:D]
    with es:
        tmp, st, gb = sb([P, NB, D]), ln_buffers(sb, sem), sb([P, 2, D])
        loaded, dve_chain, tabled, stored = (sem() for _ in range(4))
        with nc.Block() as block:
            @block.sync
            def _(sp):
                sp.dma_start(gb[:, 0], row_of(ins["L1_gnn_ln_gamma"]).broadcast_to([P, D])).then_inc(loaded, 16)
                sp.dma_start(gb[:, 1], row_of(ins["L1_gnn_ln_beta"]).broadcast_to([P, D])).then_inc(loaded, 16)
                sp.wait_ge(tabled, 1)
                sp.dma_start(table1.rearrange("(b p) d -> p b d", p=P), f).then_inc(stored, 16)
                sp.wait_ge(stored, 16)

            @block.scalar
            def _(act):
                ln_sqrt(nc, act, st, 1)
                ln_sqrt(nc, act, st, 2)

            @block.vector
            def _(dve):
                ch = Chain(dve, dve_chain)
                ln_stats(ch, None, c["x"][:], tmp, st)
                norm_nodes(ch, nc, st, c["x"][:], f)
                ch.link(nc.vector.tensor_scalar(f, f, 0.0, None, ALU.max))
                ln_stats(ch, None, f, tmp, st)
                norm_nodes(ch, nc, st, f, f)
                dve.wait_ge(loaded, 32)
                ch.link(nc.vector.tensor_tensor(f, f, bc(gb[:, 0:1], [P, NB, D]), ALU.mult))
                ch.link(nc.vector.tensor_tensor(f, f, bc(gb[:, 1:2], [P, NB, D]), ALU.add))
                dve.sem_inc(tabled, 1)


def l1_edges(nc, c, ins, blk, table1):
    es = ExitStack()
    sb = lambda shape, dt=F32: es.enter_context(nc.sbuf_tensor(fresh("buf"), shape, dt))
    sem = PhaseSemaphores(nc)
    es.callback(sem.give_back)
    agg, tab, edges = c["agg"], c["tab"], ins["edge_attr_128"]
    G = 4 * P
    with es:
        stage, xn, ea, oh = sb([P, 2, 2, HALF], I32), sb([P, 2, HALF, D]), sb([P, 2, HALF, D]), sb([P, 2, HALF, P])
        ohT, s, sT, hS, msg = sb([P, 2, G]), sb([P, 2, G]), sb([P, 4, G]), sb([P, 2, G]), sb([P, 2, G])
        w1, w2, b1, b2 = sb([D, P]), sb([P, D]), sb([P, 1]), sb([P, D])
        psH = es.enter_context(nc.psum_tensor(fresh("psum"), [P, 2, 512], F32))
        psX = es.enter_context(nc.psum_tensor(fresh("psum"), [P, 2, 512], F32))
        psS = es.enter_context(nc.psum_tensor(fresh("psum"), [P, 2, 512], F32))
        psA = es.enter_context(nc.psum_tensor(fresh("psum"), [P, 2, 512], F32))
        (loaded, staged, got0, got1, gathering, hot, ohT_ps, ohT_ready, expanded, partial, s_ready, s_act, sT_ps, sT_ready, h_ps,
         h_ready, theta_ps, biased, msg_ready, summed, added) = (sem() for _ in range(21))
        got = (got0, got1)
        with nc.Block() as block:
            @block.sync
            def _(sp):
                sp.dma_start(w1[:], ins["L1_gnn_phi_w1"]).then_inc(loaded, 16)
                sp.dma_start(w2[:], ins["L1_gnn_phi_w2"]).then_inc(loaded, 16)
                sp.dma_start(b1[:], ins["L1_gnn_phi_b1"].rearrange("(p o) -> p o", o=1)).then_inc(loaded, 16)
                sp.dma_start(b2[:], row_of(ins["L1_gnn_phi_b2"]).broadcast_to([P, D])).then_inc(loaded, 16)
                sp.wait_ge(loaded, 64)

            @block.gpsimd
            def _(pool):
                with pool.Fori(0, NH // 2) as i:
                    for h in range(2):
                        pool.wait_ge(staged, 2 * i + (h + 1))
                        pool.sem_inc(gathering, 1)
                        gather_half(nc, pool, edges, stage[:, h, 1], ea[:, h], got[h], D)
                        gather_half(nc, pool, table1, stage[:, h, 0], xn[:, h], got[h], D)

            @block.scalar
            def _(act):
                act.wait_ge(loaded, 64)
                for h in range(2):
                    nc.scalar.copy(stage[:, h, 0], c["idx"][:, h * HALF:(h + 1) * HALF])
                    nc.scalar.copy(stage[:, h, 1], c["eid"][:, h * HALF:(h + 1) * HALF]).then_inc(staged, 1)
                with act.Fori(0, NH // 2) as i:
                    for h in range(2):
                        n4 = 8 * i + 4 * h
                        for g in range(4):
                            act.wait_ge(ohT_ps, 8 * i + (4 * h + g + 1))
                            if g >= 2:
                                act.wait_ge(expanded, 8 * i + (4 * h + g - 1))
                            nc.scalar.copy(ohT[:, g % 2], psH[:, g % 2]).then_inc(ohT_ready, 1)
                        for g in range(4):
                            act.wait_ge(s_ready, 8 * i + (4 * h + g + 1))
                            nc.scalar.activation(s[:, g % 2], s[:, g % 2], ACT.Silu).then_inc(s_act, 1)
                        for g in range(4):
                            act.wait_ge(sT_ps, 8 * i + (4 * h + g + 1))
                            nc.scalar.copy(sT[:, g], psS[:, g % 2]).then_inc(sT_ready, 1)
                        for g in range(4):
                            act.wait_ge(h_ps, 8 * i + (4 * h + g + 1))
                            if g >= 2:
                                act.wait_ge(theta_ps, 8 * i + (4 * h + g - 1))
                            nc.scalar.activation(hS[:, g % 2], psH[:, g % 2], ACT.Silu, bias=b1[:]).then_inc(h_ready, 1)
                        act.wait_ge(msg_ready, 8 * i + (4 * h + 4))
                        nc.scalar.copy(stage[:, h, 0], c["idx"][:, bass.ds(half_of(i, h, 2), HALF)])
                        nc.scalar.copy(stage[:, h, 1], c["eid"][:, bass.ds(half_of(i, h, 2), HALF)]).then_inc(staged, 1)

            @block.tensor
            def _(pe):
                pe.wait_ge(loaded, 64)
                with pe.Fori(0, NH // 2) as i:
                    for h in range(2):
                        at = lambda g: 8 * i + (4 * h + g + 1)
                        blocks = pair_blocks(nc, ENG.PE, blk, i, h)

                        def expand(g):
                            pe.wait_ge(ohT_ready, at(g))
                            if g >= 2:
                                pe.wait_ge(s_ready, at(g - 2))
                            for t in range(4):
                                last = nc.tensor.matmul(psX[:, g % 2, t * P:(t + 1) * P], ohT[:, g % 2, t * P:(t + 1) * P],
                                                        flat(tab[:, bass.ds(blocks[(4 * g + t) // 2], 1), 0:D]), start=True, stop=True)
                            last.then_inc(expanded, 1)

                        def hidden(g):
                            pe.wait_ge(sT_ready, at(g))
                            nc.tensor.matmul(psH[:, g % 2], w1[:], sT[:, g], start=True, stop=True).then_inc(h_ps, 1)

                        def theta(g):
                            pe.wait_ge(h_ready, at(g))
                            for t in range(4):
                                last = nc.tensor.matmul(psX[:, g % 2, t * P:(t + 1) * P], hS[:, g % 2, t * P:(t + 1) * P], w2[:],
                                                        start=True, stop=True)
                            last.then_inc(theta_ps, 1)

                        def total(g):
                            pe.wait_ge(msg_ready, at(g))
                            if g >= 2:
                                pe.wait_ge(added, i * (2 * PAIRS) + (h * PAIRS + 2 * (g - 1) + 1))
                            for q in range(2):
                                for k in range(2):
                                    last = nc.tensor.matmul(psA[:, g % 2, q * P:(q + 1) * P], oh[:, h, 4 * g + 2 * q + k, :],
                                                            msg[:, g % 2, (2 * q + k) * P:(2 * q + k + 1) * P], start=(k == 0), stop=(k == 1))
                            last.then_inc(summed, 1)

                        pe.wait_ge(hot, 2 * i + (h + 1))
                        for g in range(4):
                            if g >= 2:
                                pe.wait_ge(ohT_ready, at(g - 2))
                            turn_onehot(nc, c, oh[:, h], psH, g).then_inc(ohT_ps, 1)
                            if g >= 1:
                                expand(g - 1)
                        expand(3)
                        for g in range(4):
                            pe.wait_ge(s_act, at(g))
                            if g >= 2:
                                pe.wait_ge(sT_ready, at(g - 2))
                            for t in range(4):
                                last = nc.tensor.transpose(psS[:, g % 2, t * P:(t + 1) * P], s[:, g % 2, t * P:(t + 1) * P], c["ident"][:])
                            last.then_inc(sT_ps, 1)
                        hidden(0)
                        hidden(1)
                        theta(0)
                        hidden(2)
                        theta(1)
                        pe.wait_ge(added, i * (2 * PAIRS) + (h * PAIRS + 1))
                        total(0)
                        hidden(3)
                        theta(2)
                        total(1)
                        theta(3)
                        total(2)
                        total(3)

            @block.vector
            def _(dve):
                nc.vector.memset(agg[:], 0.0).then_inc(added, 1)
                dve.wait_ge(loaded, 64)
                onehot(nc, c, oh[:, 0], 0).then_inc(hot, 1)
                with dve.Fori(0, NH // 2) as i:
                    for h in range(2):
                        at = lambda g: 8 * i + (4 * h + g + 1)
                        blocks = pair_blocks(nc, ENG.DVE, blk, i, h)
                        four = lambda b, g: b[:, h, 4 * g:4 * g + 4, :].rearrange("p t d -> p (t d)")

                        def message(g):
                            dve.wait_ge(theta_ps, at(g))
                            m = msg[:, g % 2].rearrange("p (t d) -> p t d", t=4)
                            nc.vector.tensor_tensor(m, psX[:, g % 2].rearrange("p (t d) -> p t d", t=4), bc(b2[:].unsqueeze(1), [P, 4, D]),
                                                    ALU.add).then_inc(biased, 1)
                            dve.wait_ge(biased, at(g))
                            nc.vector.tensor_tensor(msg[:, g % 2], msg[:, g % 2], four(xn, g), ALU.mult).then_inc(msg_ready, 1)

                        def add(g):
                            dve.wait_ge(summed, at(g))
                            for q in range(2):
                                dve.wait_ge(added, i * (2 * PAIRS) + (h * PAIRS + 2 * g + q + 1))
                                a = flat(agg[:, bass.ds(blocks[2 * g + q], 1), 0:D])
                                nc.vector.tensor_tensor(a, a, psA[:, g % 2, q * P:(q + 1) * P], ALU.add).then_inc(added, 1)

                        dve.wait_ge(got[h], 512 * i + 512)
                        for g in range(4):
                            if g >= 2:
                                dve.wait_ge(sT_ps, at(g - 2))
                            nc.vector.tensor_tensor(s[:, g % 2], four(ea, g), four(xn, g), ALU.add).then_inc(partial, 1)
                            dve.wait_ge(partial, at(g))
                            dve.wait_ge(expanded, at(g))
                            nc.vector.tensor_tensor(s[:, g % 2], s[:, g % 2], psX[:, g % 2], ALU.add).then_inc(s_ready, 1)
                        onehot(nc, c, oh[:, 1 - h], half_of(i, h, 1)).then_inc(hot, 1)
                        message(0)
                        message(1)
                        add(0)
                        message(2)
                        add(1)
                        message(3)
                        add(2)
                        add(3)


def l1_finish(nc, c, ins):
    es = ExitStack()
    sb = lambda shape, dt=F32: es.enter_context(nc.sbuf_tensor(fresh("buf"), shape, dt))
    sem = lambda: es.enter_context(nc.semaphore(fresh("sem")))
    tab, agg, x = c["tab"], c["agg"], c["x"]
    with es:
        w, b, r = sb([D, D]), sb([P, D]), sb([P, 2, D])
        m = mm_buffers(es, nc, sb, sem, 1)
        loaded, dve_chain, ready, biased = (sem() for _ in range(4))
        with nc.Block() as block:
            @block.sync
            def _(sp):
                sp.dma_start(w[:], ins["L1_gnn_theta_w"]).then_inc(loaded, 16)
                sp.dma_start(b[:], row_of(ins["L1_gnn_theta_b"]).broadcast_to([P, D])).then_inc(loaded, 16)
                sp.wait_ge(loaded, 32)

            @block.scalar
            def _(act):
                act.wait_ge(ready, 1)
                mm_scalar(act, m, lambda k, bl, stage: nc.scalar.activation(stage[:, 0, :], flat(tab[:, bass.ds(bl, 1), 0:D]), ACT.Silu))

            @block.tensor
            def _(pe):
                pe.wait_ge(loaded, 32)
                mm_tensor(nc, pe, m, c["ident"], [w[:]])

            @block.vector
            def _(dve):
                ch = Chain(dve, dve_chain)
                ch.link(nc.vector.tensor_tensor(tab[:, :, 0:D], tab[:, :, 0:D], agg[:, :, 0:D], ALU.add))
                dve.wait_ge(loaded, 32)
                ch.link(nc.vector.tensor_tensor(x[:], x[:], bc(b[:].unsqueeze(1), [P, NB, D]), ALU.add))
                dve.sem_inc(ready, 1)

                def use(bl, ps, i, k):
                    xb = flat(x[:, bass.ds(bl, 1), :])
                    nc.vector.tensor_tensor(xb, xb, ps, ALU.add).then_inc(m["consumed"], 1)
                mm_vector(nc, dve, m, use)
                dve.wait_ge(m["consumed"], NB)


def l2_nodes(nc, c):
    es = ExitStack()
    sb = lambda shape, dt=F32: es.enter_context(nc.sbuf_tensor(fresh("buf"), shape, dt))
    sem = lambda: es.enter_context(nc.semaphore(fresh("sem")))
    tab = c["tab"]
    f = tab[:, :, 0:D]
    with es:
        tmp, st = sb([P, NB, D]), ln_buffers(sb, sem)
        dve_chain, tabled, stored = (sem() for _ in range(3))
        with nc.Block() as block:
            @block.sync
            def _(sp):
                sp.wait_ge(tabled, 1)
                sp.dma_start(c["table"].rearrange("(b p) w -> p b w", p=P), tab[:]).then_inc(stored, 16)
                sp.wait_ge(stored, 16)

            @block.scalar
            def _(act):
                ln_sqrt(nc, act, st, 1)

            @block.vector
            def _(dve):
                ch = Chain(dve, dve_chain)
                ln_stats(ch, None, c["x"][:], tmp, st)
                ch.link(nc.vector.memset(tab[:, :, D:W], 1.0))
                norm_nodes(ch, nc, st, c["x"][:], f)
                ch.link(nc.vector.tensor_scalar(f, f, 0.0, None, ALU.max))
                dve.sem_inc(tabled, 1)


def l2_edges(nc, c, blk):
    es = ExitStack()
    sb = lambda shape, dt=F32: es.enter_context(nc.sbuf_tensor(fresh("buf"), shape, dt))
    sem = lambda: es.enter_context(nc.semaphore(fresh("sem")))
    agg = c["agg"]
    with es:
        stage, rows, oh = sb([P, 2, HALF], I32), sb([P, 2, HALF, W]), sb([P, 2, HALF, P])
        psA = es.enter_context(nc.psum_tensor(fresh("psum"), [P, 2, 3, 512], F32))
        staged, got0, got1, gathering, hot, summed, added = (sem() for _ in range(7))
        got = (got0, got1)
        with nc.Block() as block:
            @block.gpsimd
            def _(pool):
                with pool.Fori(0, NH // 2) as i:
                    for h in range(2):
                        pool.wait_ge(staged, 2 * i + (h + 1))
                        pool.sem_inc(gathering, 1)
                        gather_half(nc, pool, c["table"], stage[:, h], rows[:, h], got[h], W)

            @block.scalar
            def _(act):
                for h in range(2):
                    nc.scalar.copy(stage[:, h], c["idx"][:, h * HALF:(h + 1) * HALF]).then_inc(staged, 1)
                with act.Fori(0, NH // 2) as i:
                    for h in range(2):
                        act.wait_ge(summed, 2 * i + (h + 1))
                        nc.scalar.copy(stage[:, h], c["idx"][:, bass.ds(half_of(i, h, 2), HALF)]).then_inc(staged, 1)

            @block.tensor
            def _(pe):
                with pe.Fori(0, NH // 2) as i:
                    for h in range(2):
                        pe.wait_ge(hot, 2 * i + (h + 1))
                        pe.wait_ge(got[h], 256 * i + 256)
                        sum_pairs(nc, psA[:, h], oh[:, h], rows[:, h], D + 1).then_inc(summed, 1)

            @block.vector
            def _(dve):
                nc.vector.memset(agg[:], 0.0).then_inc(added, 1)
                onehot(nc, c, oh[:, 0], 0).then_inc(hot, 1)
                with dve.Fori(0, NH // 2) as i:
                    for h in range(2):
                        dve.wait_ge(added, i * (2 * PAIRS) + (h * PAIRS + 1))
                        onehot(nc, c, oh[:, 1 - h], half_of(i, h, 1)).then_inc(hot, 1)
                        blocks = pair_blocks(nc, ENG.DVE, blk, i, h)
                        dve.wait_ge(summed, 2 * i + (h + 1))
                        add_pairs(nc, dve, agg, psA[:, h], blocks, D + 1, added, i, h)


def l2_finish(nc, c, ins):
    es = ExitStack()
    sb = lambda shape, dt=F32: es.enter_context(nc.sbuf_tensor(fresh("buf"), shape, dt))
    sem = lambda: es.enter_context(nc.semaphore(fresh("sem")))
    tab, agg, x = c["tab"], c["agg"], c["x"]
    o, mean = tab[:, :, 0:D], agg[:, :, 0:D]
    sh = [P, NB, D]
    with es:
        wl, wr, bl, br = sb([D, D]), sb([D, D]), sb([P, D]), sb([P, D])
        deg, sq, nrm = sb([P, NB]), sb([P, NB]), sb([P, NB])
        m = mm_buffers(es, nc, sb, sem, 2)
        loaded, dve_chain, ready, squared, rooted = (sem() for _ in range(5))
        with nc.Block() as block:
            @block.sync
            def _(sp):
                for d, s in ((wl, ins["L2_gnn_Wl"]), (wr, ins["L2_gnn_Wr"]), (bl, row_of(ins["L2_gnn_bl"]).broadcast_to([P, D])),
                             (br, row_of(ins["L2_gnn_br"]).broadcast_to([P, D]))):
                    sp.dma_start(d[:], s).then_inc(loaded, 16)
                sp.wait_ge(loaded, 64)

            @block.scalar
            def _(act):
                act.wait_ge(ready, 1)

                def fill(k, b, stage):
                    nc.scalar.copy(stage[:, 0, :], flat(tab[:, bass.ds(b, 1), 0:D]))
                    return nc.scalar.copy(stage[:, 1, :], flat(agg[:, bass.ds(b, 1), 0:D]))
                mm_scalar(act, m, fill)
                act.wait_ge(squared, 1)
                nc.scalar.activation(nrm[:], sq[:], ACT.Sqrt).then_inc(rooted, 1)

            @block.tensor
            def _(pe):
                pe.wait_ge(loaded, 64)
                mm_tensor(nc, pe, m, c["ident"], [wl[:], wr[:]])

            @block.vector
            def _(dve):
                ch = Chain(dve, dve_chain)
                ch.link(nc.vector.tensor_scalar(deg[:].unsqueeze(2), agg[:, :, D:D + 1], 1.0, None, ALU.max))
                ch.link(nc.vector.reciprocal(deg[:], deg[:]))
                ch.link(nc.vector.tensor_tensor(mean, mean, bc(deg[:].unsqueeze(2), sh), ALU.mult))
                dve.wait_ge(loaded, 64)
                ch.link(nc.vector.tensor_tensor(bl[:], bl[:], br[:], ALU.add))
                dve.sem_inc(ready, 1)

                def use(b, ps, i, k):
                    nc.vector.tensor_tensor(flat(tab[:, bass.ds(b, 1), 0:D]), ps, bl[:], ALU.add).then_inc(m["consumed"], 1)
                mm_vector(nc, dve, m, use)
                dve.wait_ge(m["consumed"], NB)
                ch.link(nc.vector.tensor_scalar(o, o, 0.0, None, ALU.max))
                ch.link(nc.vector.tensor_tensor(mean, o, o, ALU.mult))
                nc.vector.tensor_reduce(sq[:], mean, AX.X, ALU.add).then_inc(squared, 1)
                dve.wait_ge(rooted, 1)
                ch.link(nc.vector.tensor_scalar(nrm[:], nrm[:], 1e-6, None, ALU.add))
                ch.link(nc.vector.reciprocal(nrm[:], nrm[:]))
                ch.link(nc.vector.tensor_tensor(o, o, bc(nrm[:].unsqueeze(2), sh), ALU.mult))
                ch.link(nc.vector.tensor_tensor(x[:], x[:], o, ALU.add))


SLOPE = 0.2


def heads(ap):
    return ap.rearrange("p t (h k) -> p t h k", h=HEADS)


def l3_nodes(nc, c, ins, seg):
    es = ExitStack()
    sb = lambda shape, dt=F32: es.enter_context(nc.sbuf_tensor(fresh("buf"), shape, dt))
    sem = lambda: es.enter_context(nc.semaphore(fresh("sem")))
    tab = c["tab"]
    with es:
        tmp, st, m = sb([P, NB, D]), ln_buffers(sb, sem), mm_buffers(es, nc, sb, sem, 1)
        w, wT, att, low = sb([D, D]), sb([D, D]), sb([P, 2, D]), sb([1, HEADS])
        psW = es.enter_context(nc.psum_tensor(fresh("psum"), [P, 512], F32))
        loaded, stats, dve_chain, tabled, stored, w_turned, w_ready = (sem() for _ in range(7))
        with nc.Block() as block:
            @block.sync
            def _(sp):
                sp.dma_start(w[:], ins["L3_gnn_W"]).then_inc(loaded, 16)
                for k, name in enumerate(("L3_gnn_att_src", "L3_gnn_att_dst")):
                    sp.dma_start(att[:, k], ins[name].rearrange("o h k -> o (h k)").broadcast_to([P, D])).then_inc(loaded, 16)
                sp.wait_ge(tabled, 1)
                sp.dma_start(c["table"].rearrange("(b p) w -> p b w", p=P), tab[:]).then_inc(stored, 16)
                sp.wait_ge(stored, 16)
                sp.dma_start(c["table"][DUMMY:DUMMY + 1, D:W], low[:]).then_inc(stored, 16)
                sp.wait_ge(stored, 32)

            @block.scalar
            def _(act):
                ln_sqrt(nc, act, st, 1)
                act.wait_ge(stats, 1)
                mm_scalar(act, m, lambda k, b, stage: nc.scalar.activation(
                    stage[:, 0, :], flat(c["x"][:, bass.ds(b, 1), :]), ACT.Relu,
                    bias=st["nmr"][:, bass.ds(b, 1)], scale=st["rstd"][:, bass.ds(b, 1)]))

            @block.tensor
            def _(pe):
                pe.wait_ge(loaded, 48)
                nc.tensor.transpose(psW[:, 0:D], w[:], c["ident"][:]).then_inc(w_turned, 1)
                pe.wait_ge(w_ready, 1)
                mm_tensor(nc, pe, m, c["ident"], [wT[:]])

            @block.vector
            def _(dve):
                ch = Chain(dve, dve_chain)
                nc.vector.memset(low[:], NEG)
                dve.wait_ge(w_turned, 1)
                nc.vector.tensor_copy(wT[:], psW[:, 0:D]).then_inc(w_ready, 1)
                ln_stats(ch, None, c["x"][:], tmp, st)
                dve.sem_inc(stats, 1)
                dve.wait_ge(loaded, 48)
                mm_vector(nc, dve, m, lambda b, ps, i, k: nc.vector.tensor_copy(
                    flat(tab[:, bass.ds(b, 1), 0:D]), ps).then_inc(m["consumed"], 1))
                dve.wait_ge(m["consumed"], NB)
                for k, score in enumerate((tab[:, :, D:W], seg[:, :, 0:HEADS])):
                    ch.link(nc.vector.tensor_tensor(tmp[:], tab[:, :, 0:D], bc(att[:, k:k + 1], [P, NB, D]), ALU.mult))
                    ch.link(nc.vector.tensor_reduce(score, heads(tmp[:]), AX.X, ALU.add))
                ch.link(nc.vector.tensor_copy(seg[:, :, HEADS:], tab[:, :, D:W]))
                dve.sem_inc(tabled, 1)


def l3_max(nc, c, blk, seg):
    es = ExitStack()
    sb = lambda shape, dt=F32: es.enter_context(nc.sbuf_tensor(fresh("buf"), shape, dt))
    sem = lambda: es.enter_context(nc.semaphore(fresh("sem")))
    K = HALF // 2 * HEADS
    with es:
        stage, rows, oh = sb([P, 2, HALF], I32), sb([P, 2, HALF, W]), sb([P, 2, HALF, P])
        ohT = sb([P, 2, 4 * P], BF16)
        packed, packedT = sb([P, 2, P]), sb([P, 2, P], BF16)
        pick, bar, picks = sb([P, K, P], BF16), sb([P, P], BF16), sb([P, K])
        part, rest = sb([P, 2, K], BF16), sb([P, 2, K])
        best = sb([P, PAIRS, HEADS])
        psT = es.enter_context(nc.psum_tensor(fresh("psum"), [P, 2, 512], F32))
        psK = es.enter_context(nc.psum_tensor(fresh("psum"), [P, 512], F32))
        psQ = es.enter_context(nc.psum_tensor(fresh("psum"), [P, 2, 2, 512], F32))
        (staged, got0, got1, gathering, saved0, saved1, hot, packs, pack_ps, pack_ready, ohT_ps, ohT_ready, scored, reduced, maxed,
         consts, cleared, split) = (sem() for _ in range(18))
        got, saved = (got0, got1), (saved0, saved1)
        with nc.Block() as block:
            @block.sync
            def _(sp):
                with sp.Fori(0, NH // 2) as i:
                    for h in range(2):
                        sp.wait_ge(got[h], 256 * i + 256)
                        sp.dma_start(c["kept"][bass.ds(2 * i + h, 1)].rearrange("o p w -> (o p) w"),
                                     rows[:, h].rearrange("p t w -> p (t w)")).then_inc(saved[h], 16)
                sp.wait_ge(saved0, 16 * (NH // 2))
                sp.wait_ge(saved1, 16 * (NH // 2))

            @block.gpsimd
            def _(pool):
                with pool.Fori(0, NH // 2) as i:
                    for h in range(2):
                        pool.wait_ge(staged, 2 * i + (h + 1))
                        pool.sem_inc(gathering, 1)
                        gather_half(nc, pool, c["table"], stage[:, h], rows[:, h], got[h], W)

            @block.scalar
            def _(act):
                for h in range(2):
                    nc.scalar.copy(stage[:, h], c["idx"][:, h * HALF:(h + 1) * HALF]).then_inc(staged, 1)
                with act.Fori(0, NH // 2) as i:
                    for h in range(2):
                        act.wait_ge(pack_ps, 2 * i + (h + 1))
                        nc.scalar.copy(flat(packedT[:]), psK[:, 0:2 * P]).then_inc(pack_ready, 1)
                        for g in range(4):
                            act.wait_ge(ohT_ps, 8 * i + (4 * h + g + 1))
                            if g >= 2:
                                act.wait_ge(scored, i * (2 * PAIRS) + (h * PAIRS + 2 * (g - 1)))
                            nc.scalar.copy(ohT[:, g % 2], psT[:, g % 2]).then_inc(ohT_ready, 1)
                        act.wait_ge(saved[h], 16 * i + 16)
                        nc.scalar.copy(stage[:, h], c["idx"][:, bass.ds(half_of(i, h, 2), HALF)]).then_inc(staged, 1)

            @block.tensor
            def _(pe):
                pe.wait_ge(consts, 1)
                with pe.Fori(0, NH // 2) as i:
                    for h in range(2):
                        def score(g):
                            pe.wait_ge(ohT_ready, 8 * i + (4 * h + g + 1))
                            for q in (2 * g, 2 * g + 1):
                                if q >= 2:
                                    pe.wait_ge(reduced, i * (2 * PAIRS) + (h * PAIRS + q - 1))
                                for s in range(2):
                                    t = 2 * q + s
                                    o = psQ[:, q % 2, s, :]
                                    e = ohT[:, g % 2, (t % 4) * P:(t % 4 + 1) * P]
                                    nc.tensor.matmul(o.rearrange("p (k e) -> p k e", k=HEADS), bar[:], bc(e.unsqueeze(1), [P, HEADS, P]),
                                                     start=True, stop=False)
                                    for k in range(HEADS):
                                        last = nc.tensor.matmul(o[:, k * P:(k + 1) * P], pick[:, (t % 8) * HEADS + k, :], packedT[:, t // 8, :],
                                                                start=False, stop=(k == HEADS - 1))
                                last.then_inc(scored, 1)

                        pe.wait_ge(packs, 2 * i + (h + 1))
                        pe.wait_ge(hot, 2 * i + (h + 1))
                        nc.tensor.transpose(psK[:, 0:P], packed[:, 0], c["ident"][:])
                        nc.tensor.transpose(psK[:, P:2 * P], packed[:, 1], c["ident"][:]).then_inc(pack_ps, 1)
                        for g in range(4):
                            if g >= 2:
                                pe.wait_ge(ohT_ready, 8 * i + (4 * h + g - 1))
                            turn_onehot(nc, c, oh[:, h], psT, g).then_inc(ohT_ps, 1)
                            if g == 0:
                                pe.wait_ge(pack_ready, 2 * i + (h + 1))
                            else:
                                score(g - 1)
                        score(3)

            @block.vector
            def _(dve):
                nc.vector.memset(packed[:], 0.0).then_inc(cleared, 1)
                dve.wait_ge(cleared, 1)
                ch = Chain(dve, cleared, start=1)
                ch.link(nc.vector.tensor_tensor(picks[:], c["ident"][:, 0:K], c["ident"][:, K:2 * K], ALU.add))
                ch.link(nc.vector.tensor_tensor(picks[:], picks[:], c["ident"][:, 2 * K:3 * K], ALU.add))
                ch.link(nc.vector.tensor_copy(pick[:], bc(picks[:].unsqueeze(2), [P, K, P])))
                nc.vector.tensor_scalar(bar[:], c["ident"][:], -1.0, BIG, ALU.add, ALU.mult).then_inc(consts, 1)
                dve.sem_inc(maxed, 1)
                onehot(nc, c, oh[:, 0], 0).then_inc(hot, 1)
                with dve.Fori(0, NH // 2) as i:
                    for h in range(2):
                        dve.wait_ge(got[h], 256 * i + 256)
                        lp = Chain(dve, split, start=10 * i + 5 * h)
                        sc = rows[:, h, :, D:W].rearrange("p (g t) k -> p g t k", g=2)
                        as_t = lambda b: b.rearrange("p g (t k) -> p g t k", k=HEADS)
                        lp.link(nc.vector.tensor_copy(as_t(part[:]), sc))
                        nc.vector.tensor_copy(packed[:, :, 0:K], part[:])
                        lp.link(nc.vector.tensor_tensor(as_t(rest[:]), sc, as_t(part[:]), ALU.subtract))
                        lp.link(nc.vector.tensor_copy(part[:], rest[:]))
                        nc.vector.tensor_copy(packed[:, :, K:2 * K], part[:])
                        lp.link(nc.vector.tensor_tensor(rest[:], rest[:], part[:], ALU.subtract))
                        lp.link(nc.vector.tensor_copy(part[:], rest[:]))
                        nc.vector.tensor_copy(packed[:, :, 2 * K:3 * K], part[:]).then_inc(packs, 1)
                        onehot(nc, c, oh[:, 1 - h], half_of(i, h, 1)).then_inc(hot, 1)
                        blocks = pair_blocks(nc, ENG.DVE, blk, i, h)
                        def keep(q):
                            dve.wait_ge(reduced, i * (2 * PAIRS) + (h * PAIRS + q + 1))
                            dve.wait_ge(maxed, i * (2 * PAIRS) + (h * PAIRS + q + 1))
                            a = flat(seg[:, bass.ds(blocks[q], 1), HEADS:])
                            nc.vector.tensor_tensor(a, a, best[:, q], ALU.max).then_inc(maxed, 1)

                        for q in range(PAIRS):
                            dve.wait_ge(scored, i * (2 * PAIRS) + (h * PAIRS + q + 1))
                            nc.vector.tensor_reduce(best[:, q], psQ[:, q % 2].rearrange("p s (k e) -> p k s e", k=HEADS),
                                                    AX.XY, ALU.max).then_inc(reduced, 1)
                            if q:
                                keep(q - 1)
                        keep(PAIRS - 1)


def l3_self(nc, c, seg):
    es = ExitStack()
    sb = lambda shape, dt=F32: es.enter_context(nc.sbuf_tensor(fresh("buf"), shape, dt))
    sem = lambda: es.enter_context(nc.semaphore(fresh("sem")))
    tab, agg = c["tab"], c["agg"]
    ad, mx, a_src = seg[:, :, 0:HEADS], seg[:, :, HEADS:], tab[:, :, D:W]
    with es:
        z = sb([P, NB, HEADS])
        dve_chain, ready, weights = (sem() for _ in range(3))
        with nc.Block() as block:
            @block.scalar
            def _(act):
                act.wait_ge(ready, 1)
                nc.scalar.activation(agg[:, :, D:W], z[:], ACT.Exp).then_inc(weights, 1)

            @block.vector
            def _(dve):
                ch = Chain(dve, dve_chain)
                ch.link(nc.vector.tensor_tensor(mx, mx, ad, ALU.add))
                ch.link(nc.vector.scalar_tensor_tensor(mx, mx, SLOPE, mx, ALU.mult, ALU.max))
                ch.link(nc.vector.tensor_tensor(z[:], a_src, ad, ALU.add))
                ch.link(nc.vector.scalar_tensor_tensor(z[:], z[:], SLOPE, z[:], ALU.mult, ALU.max))
                nc.vector.tensor_tensor(z[:], z[:], mx, ALU.subtract).then_inc(ready, 1)
                dve.wait_ge(weights, 1)
                ch.link(nc.vector.tensor_tensor(heads(agg[:, :, 0:D]), heads(tab[:, :, 0:D]),
                                                bc(agg[:, :, D:W].unsqueeze(3), [P, NB, HEADS, HEAD_DIM]), ALU.mult))


def l3_edges(nc, c, blk, seg):
    es = ExitStack()
    sb = lambda shape, dt=F32: es.enter_context(nc.sbuf_tensor(fresh("buf"), shape, dt))
    sem = lambda: es.enter_context(nc.semaphore(fresh("sem")))
    agg, S = c["agg"], 2 * HEADS
    with es:
        rows, oh, ohT = sb([P, 2, HALF, W]), sb([P, 2, HALF, P]), sb([P, 2, 4 * P])
        z = sb([P, HALF, HEADS])
        psT = es.enter_context(nc.psum_tensor(fresh("psum"), [P, 2, 512], F32))
        psE = es.enter_context(nc.psum_tensor(fresh("psum"), [P, HALF, S], F32))
        psA = es.enter_context(nc.psum_tensor(fresh("psum"), [P, 3, 512], F32))
        (back0, back1, hot, ohT_ps, ohT_ready, expanded, dve_chain, zed, weights, weighted, summed, added) = (sem() for _ in range(12))
        back = (back0, back1)
        DV = 2
        with nc.Block() as block:
            @block.sync
            def _(sp):
                def load(n, h):
                    sp.dma_start(rows[:, h].rearrange("p t w -> p (t w)"), c["kept"][n].rearrange("o p w -> (o p) w")).then_inc(back[h], 16)
                load(slice(0, 1), 0)
                load(slice(1, 2), 1)
                with sp.Fori(0, NH // 2 - 1) as i:
                    for h in range(2):
                        sp.wait_ge(summed, 2 * i + (h + 1))
                        load(bass.ds(2 * i + (h + 2), 1), h)

            @block.scalar
            def _(act):
                def weigh(n, h):
                    for g in range(4):
                        act.wait_ge(ohT_ps, 4 * n + (g + 1))
                        if g >= 2:
                            act.wait_ge(expanded, 4 * n + (g - 1))
                        nc.scalar.copy(ohT[:, g % 2], psT[:, g % 2]).then_inc(ohT_ready, 1)
                    act.wait_ge(zed, n + 1)
                    nc.scalar.activation(rows[:, h, :, D:W], z[:], ACT.Exp).then_inc(weights, 1)
                weigh(0, 0)
                with act.Fori(0, NH // 2 - 1) as i:
                    for h in range(2):
                        weigh(2 * i + (h + 1), 1 - h)
                weigh(NH - 1, 1)

            @block.tensor
            def _(pe):
                def spread(n, h, blocks):
                    def expand(g):
                        pe.wait_ge(ohT_ready, 4 * n + (g + 1))
                        for t in range(4 * g, 4 * g + 4):
                            last = nc.tensor.matmul(psE[:, t, :], ohT[:, g % 2, (t % 4) * P:(t % 4 + 1) * P],
                                                    flat(seg[:, bass.ds(blocks[t // 2], 1), :]), start=True, stop=True)
                        last.then_inc(expanded, 1)
                    pe.wait_ge(hot, n + 1)
                    for g in range(4):
                        if g >= 2:
                            pe.wait_ge(ohT_ready, 4 * n + (g - 1))
                        turn_onehot(nc, c, oh[:, h], psT, g).then_inc(ohT_ps, 1)
                        if g >= 1:
                            expand(g - 1)
                    expand(3)

                def total(i, h):
                    pe.wait_ge(weighted, 2 * i + (h + 1))
                    pe.wait_ge(added, i * (2 * PAIRS) + (h * PAIRS + 1))
                    sum_pairs(nc, psA, oh[:, h], rows[:, h], W).then_inc(summed, 1)

                spread(0, 0, pair_blocks(nc, ENG.PE, blk, 0, 0))
                with pe.Fori(0, NH // 2 - 1) as i:
                    for h in range(2):
                        total(i, h)
                        spread(2 * i + (h + 1), 1 - h, pair_blocks(nc, ENG.PE, blk, i, h, 1))
                total(NH // 2 - 1, 0)
                spread(NH - 1, 1, pair_blocks(nc, ENG.PE, blk, NH // 2 - 1, 0, 1))
                total(NH // 2 - 1, 1)

            @block.vector
            def _(dve):
                def weigh(n, h, rows_at):
                    lp = Chain(dve, dve_chain, start=n * DV)
                    dve.wait_ge(expanded, 4 * n + 4)
                    dve.wait_ge(back[h], rows_at)
                    lp.link(nc.vector.tensor_tensor(z[:], psE[:, :, 0:HEADS], rows[:, h, :, D:W], ALU.add))
                    lp.link(nc.vector.scalar_tensor_tensor(z[:], z[:], SLOPE, z[:], ALU.mult, ALU.max))
                    nc.vector.tensor_tensor(z[:], z[:], psE[:, :, HEADS:], ALU.subtract).then_inc(zed, 1)
                    dve.wait_ge(weights, n + 1)
                    r = heads(rows[:, h, :, 0:D])
                    nc.vector.tensor_tensor(r, r, bc(rows[:, h, :, D:W].unsqueeze(3), [P, HALF, HEADS, HEAD_DIM]), ALU.mult).then_inc(weighted, 1)
                    assert lp.n == DV

                def add(i, h):
                    blocks = pair_blocks(nc, ENG.DVE, blk, i, h)
                    dve.wait_ge(summed, 2 * i + (h + 1))
                    add_pairs(nc, dve, agg, psA, blocks, W, added, i, h)

                dve.sem_inc(added, 1)
                onehot(nc, c, oh[:, 0], 0).then_inc(hot, 1)
                weigh(0, 0, 16)
                with dve.Fori(0, NH // 2 - 1) as i:
                    for h in range(2):
                        onehot(nc, c, oh[:, 1 - h], half_of(i, h, 1)).then_inc(hot, 1)
                        add(i, h)
                        weigh(2 * i + (h + 1), 1 - h, 16 * i + 16 + 16 * h)
                onehot(nc, c, oh[:, 1], half_of(NH // 2 - 1, 0, 1)).then_inc(hot, 1)
                add(NH // 2 - 1, 0)
                weigh(NH - 1, 1, 16 * (NH // 2))
                add(NH // 2 - 1, 1)


def l3_finish(nc, c, ins):
    agg, x = c["agg"], c["x"]
    with (nc.sbuf_tensor("l3_bias", [P, D], F32) as bias, nc.sbuf_tensor("l3_inverse", [P, NB, HEADS], F32) as inv,
          nc.semaphore("l3_loaded") as loaded, nc.semaphore("l3_chain") as dve_chain, nc.Block() as block):
        @block.sync
        def _(sp):
            sp.dma_start(bias[:], row_of(ins["L3_gnn_bias"]).broadcast_to([P, D])).then_inc(loaded, 16)

        @block.vector
        def _(dve):
            ch = Chain(dve, dve_chain)
            ch.link(nc.vector.reciprocal(inv[:], agg[:, :, D:W]))
            ch.link(nc.vector.tensor_tensor(heads(agg[:, :, 0:D]), heads(agg[:, :, 0:D]),
                                            bc(inv[:].unsqueeze(3), [P, NB, HEADS, HEAD_DIM]), ALU.mult))
            ch.link(nc.vector.tensor_tensor(x[:], x[:], agg[:, :, 0:D], ALU.add))
            dve.wait_ge(loaded, 16)
            ch.link(nc.vector.tensor_tensor(x[:], x[:], bc(bias[:].unsqueeze(1), [P, NB, D]), ALU.add))


_INS = ["x", "src", "dst", "edge_attr_128", "L0_gnn_W_w", "L0_gnn_W_b", "L0_gnn_a_w", "L0_gnn_a_b", "L1_gnn_ln_gamma",
        "L1_gnn_ln_beta", "L1_gnn_phi_w1", "L1_gnn_phi_b1", "L1_gnn_phi_w2", "L1_gnn_phi_b2", "L1_gnn_theta_w",
        "L1_gnn_theta_b", "L2_gnn_Wl", "L2_gnn_bl", "L2_gnn_Wr", "L2_gnn_br", "L3_gnn_W", "L3_gnn_att_src",
        "L3_gnn_att_dst", "L3_gnn_bias"]


def kernel(**inputs):
    import numpy as np
    import concourse.bacc as bacc
    from concourse.bass_utils import run_bass_kernel_spmd as run

    nc = bacc.Bacc("TRN2", target_bir_lowering=False, num_devices=1)
    arrays, aps = {}, {}
    for name in _INS:
        a = np.ascontiguousarray(inputs[name])
        arrays[f"in_{name}"] = a
        aps[name] = nc.dram_tensor(f"in_{name}", a.shape, mybir.dt.from_np(a.dtype), kind="ExternalInput").ap()
    out = nc.dram_tensor("out_x", (N, D), F32, kind="ExternalOutput").ap()
    gnn_kernel(nc, aps, out)
    r = run(nc, [arrays], core_ids=[0])
    return r.results[0]["out_x"]
```

```python
import concourse.bass as bass
from concourse import mybir
from contextlib import ExitStack

F32 = mybir.dt.float32
I32 = mybir.dt.int32
BF16 = mybir.dt.bfloat16
ALU = mybir.AluOpType
ACT = mybir.ActivationFunctionType
AX = mybir.AxisListType
ENG = mybir.EngineType

P = 128
N, E, D = 6250, 206250, 128
HEADS, HEAD_DIM = 4, 32
NB = -(-N // P)
NP = NB * P
LAST = N - (NB - 1) * P
DUMMY = NP - 1
HALF = 16
PAIRS = HALF // 2
ET = 1616
E_LAST = E - (P - 1) * ET
NPAIR = -(-((E + NB * (2 * P - 1)) // (2 * P)) // (2 * PAIRS)) * 2 * PAIRS
NT = 2 * NPAIR
NH = NT // HALF
NTX = NT + 4 * HALF
SLOTS = NT * P
PAYC = NTX
W = 132
NBLK = NB + 1
EMPTY_DST = NB * P
NEG = -1.0e30
BIG = 2.0 ** 100
LN_EPS = 1e-5
assert (P * ET - E) <= HALF * P and NH % 2 == 0
BLOCK_RANGE = "block numbers are clamped to 0..NB-1 where they are made"


_names = [0]


def fresh(kind):
    _names[0] += 1
    return f"{kind}_{_names[0]}"


class PhaseSemaphores:

    def __init__(self, nc):
        self.nc, self.taken = nc, []

    def __call__(self):
        self.taken.append(self.nc.alloc_semaphore(fresh("sem")))
        return self.taken[-1]

    def give_back(self):
        self.nc.clear_and_free_semaphores(self.taken)
        self.nc.all_engine_barrier()


class Chain:

    def __init__(self, eng, sem, start=0):
        self.eng, self.sem, self.n, self.start = eng, sem, 0, start

    def link(self, ins):
        self.n += 1
        ins.then_inc(self.sem, 1)
        self.eng.wait_ge(self.sem, self.start + self.n)


def bc(ap, shape):
    return ap.broadcast_to(shape)


def flat(ap):
    return ap.rearrange("p a b -> p (a b)")


def gnn_kernel(nc, ins, out):
    es = ExitStack()
    sb = lambda shape, dt=F32: es.enter_context(nc.sbuf_tensor(fresh("buf"), shape, dt))
    dram = lambda name, shape, dt=F32: nc.dram_tensor(name, shape, dt).ap()

    pay_a = dram("payload_by_src", (P * PAYC, 4), I32)
    pay_b = dram("payload_by_dst", (P * PAYC, 4), I32)
    listed = dram("records_as_listed", (P * ET, 4), I32)
    table = dram("node_rows", (NP, W))
    table1 = dram("node_rows_ln", (NP, D))

    with es:
        x_sb = sb([P, NB, D])
        iota = sb([P, P])
        ident = sb([P, P])
        ones = sb([P, P])
        idx = sb([P, NTX], I32)
        eid = sb([P, NTX], I32)
        loc = sb([P, NTX])
        blk_a = sb([1, NPAIR + 2 * PAIRS], I32)
        blk_b = sb([1, NPAIR + 2 * PAIRS], I32)

        sort_phase(nc, ins, x_sb, iota, ident, ones, pay_a, pay_b, blk_a, blk_b, listed)

        agg = sb([P, NB, W])
        tab = sb([P, NB, W])
        load_order(nc, pay_a, idx, eid, loc)
        c = dict(iota=iota, ident=ident, ones=ones, idx=idx, eid=eid, loc=loc, agg=agg, tab=tab, x=x_sb, table=table)

        with nc.sbuf_tensor([P, NB, 1], F32) as a_src:
            l0_nodes(nc, c, ins, a_src)
            l0_edges(nc, c, ins, blk_a, a_src)
        l0_finish(nc, c)
        l1_nodes(nc, c, ins, table1)
        l1_edges(nc, c, ins, blk_a, table1)
        l1_finish(nc, c, ins)
        l2_nodes(nc, c)
        l2_edges(nc, c, blk_a)
        l2_finish(nc, c, ins)
        first, fence = (eid[:, k * (NPAIR + 2 * PAIRS):(k + 1) * (NPAIR + 2 * PAIRS)].bitcast(F32) for k in range(2))
        load_order_by_dst(nc, pay_b, ones, blk_b, idx, loc, first, fence)
        with nc.sbuf_tensor([P, NB, 2 * HEADS], F32) as seg:
            l3_nodes(nc, c, ins, seg)
            l3_edges(nc, c, blk_b, seg, first, fence)
        l3_finish(nc, c, ins)
        store_phase(nc, x_sb, out)


def sort_phase(nc, ins, x_sb, iota, ident, ones, pay_a, pay_b, blk_a, blk_b, listed):
    es = ExitStack()
    sb = lambda shape, dt=F32: es.enter_context(nc.sbuf_tensor(fresh("buf"), shape, dt))
    sem = PhaseSemaphores(nc)
    es.callback(sem.give_back)
    G = HALF // 2
    with es:
        src, dst, eno = sb([P, ET], I32), sb([P, ET], I32), sb([P, ET], I32)
        after = sb([P, ET], I32)
        falls, unsorted = sb([P, 1]), sb([1, 1], I32)
        gain, qstep = sb([P, NBLK]), sb([1, NPAIR + 2 * PAIRS])
        qrun, qfrom = sb([1, NPAIR + 2 * PAIRS]), sb([1, NPAIR + 2 * PAIRS], I32)
        blkf, mask, scan, pos = sb([P, ET], BF16), sb([P, ET], BF16), sb([P, ET]), sb([P, ET])
        place = sb([P, ET])
        addr = [sb([P, ET], I32), sb([P, ET], I32)]
        pay = [sb([P, ET, 4], I32)]
        pay.append(sb([P, ET, 4], I32))
        empty = sb([P, PAYC // 4, 4], I32)
        below, bno = sb([P, P]), sb([P, NBLK])
        cnt, off, pairs_f, cum, zero = (sb([P, NBLK]) for _ in range(5))
        pairs_i = sb([P, NBLK], I32)
        qno, qblk = sb([1, NPAIR + 2 * PAIRS]), sb([1, NPAIR + 2 * PAIRS])
        pos_st, pay_st = sb([P, 2, G], I32), sb([P, 2, G, 4], I32)
        ps = es.enter_context(nc.psum_tensor(fresh("psum"), [P, 3, 512], F32))
        loaded, made, filled, dve_chain, pool_chain, counted, prefixed, ranked = (sem() for _ in range(8))
        staged, slot_free, out0, out1 = (sem() for _ in range(4))
        rank_a, rank_b, scattering, consts = sem(), sem(), sem(), sem()
        recorded, in_dram, ran, counted_falls, fell, run_known = (sem() for _ in range(6))
        assert PAYC % 4 == 0 and ET % (2 * G) == 0

        with nc.Block() as block:
            @block.sync
            def _(sp):
                sp.wait_ge(made, 1)
                for b, e in ((src, ins["src"]), (dst, ins["dst"])):
                    sp.dma_start(b[0:P - 1, :], e[0:(P - 1) * ET].rearrange("(p t) -> p t", t=ET)).then_inc(loaded, 16)
                    sp.dma_start(b[P - 1:P, 0:E_LAST], e[(P - 1) * ET:E].rearrange("(p t) -> p t", p=1)).then_inc(loaded, 16)
                sp.dma_start(after[0:P - 1, :], ins["dst"][1:1 + (P - 1) * ET].rearrange("(p t) -> p t", t=ET)).then_inc(loaded, 16)
                sp.dma_start(after[P - 1:P, 0:E_LAST - 1], ins["dst"][1 + (P - 1) * ET:E].rearrange("(p t) -> p t", p=1)).then_inc(loaded, 16)
                sp.dma_start(x_sb[:, 0:NB - 1, :], ins["x"][0:(NB - 1) * P, :].rearrange("(b p) d -> p b d", p=P)).then_inc(loaded, 16)
                sp.dma_start(x_sb[0:LAST, NB - 1, :], ins["x"][(NB - 1) * P:N, :]).then_inc(loaded, 16)
                sp.wait_ge(made, 2)
                for o in (pay_a, pay_b):
                    v = o.rearrange("(p t) c -> p (t c)", p=P)
                    for k in range(4):
                        sp.dma_start(v[:, k * PAYC:(k + 1) * PAYC], empty[:].rearrange("p t c -> p (t c)")).then_inc(filled, 16)
                sp.wait_ge(recorded, 1)
                sp.dma_start(listed.rearrange("(p t) c -> p (t c)", t=ET), pay[1][:].rearrange("p t c -> p (t c)")).then_inc(in_dram, 16)
                sp.wait_ge(in_dram, 16)
                sp.wait_ge(filled, 8 * 16)
                sp.wait_ge(run_known, 1)
                slots = pay_b.rearrange("(p t) c -> p t c", p=P)
                scattered = sp.value_load(unsorted[0:1, 0:1], min_val=0, max_val=1)
                with sp.If(1 - scattered):
                    with sp.Fori(0, NPAIR // PAIRS) as i:
                        starts = nc.values_load_multi_w_load_instructions(
                            qfrom[0:1, bass.ds(i * PAIRS, PAIRS)], engines=[ENG.SP], min_val=0, max_val=E,
                            skip_runtime_bounds_check_because="the starts are clamped to 0..E where they are made")[1]
                        for q in range(PAIRS):
                            sp.dma_start(slots[:, bass.ds(i * (2 * PAIRS) + 2 * q, 2), :],
                                         listed[bass.ds(starts[q], 2 * P), :].rearrange("(p s) c -> p s c", s=2)).then_inc(ran, 16)
                    sp.wait_ge(ran, 16 * NPAIR)

            @block.gpsimd
            def _(pool):
                ch = Chain(pool, pool_chain)
                nc.gpsimd.iota(eno[:], [[1, ET]], base=0, channel_multiplier=ET)
                nc.gpsimd.iota(iota[:], [[1, P]], base=0, channel_multiplier=0, allow_small_or_imprecise_dtypes=True)
                nc.gpsimd.iota(bno[:], [[1, NBLK]], base=0, channel_multiplier=0, allow_small_or_imprecise_dtypes=True)
                nc.gpsimd.iota(qno[:], [[1, NPAIR + 2 * PAIRS]], base=0, channel_multiplier=0, allow_small_or_imprecise_dtypes=True)
                nc.gpsimd.memset(ones[:], 1.0)
                ch.link(nc.gpsimd.memset(ident[:], 0.0))
                ch.link(nc.gpsimd.affine_select(out=ident[:], in_=ident[:], compare_op=ALU.not_equal, fill=1.0, base=0,
                                                pattern=[[-1, P]], channel_multiplier=1))
                ch.link(nc.gpsimd.memset(below[:], 0.0))
                ch.link(nc.gpsimd.affine_select(out=below[:], in_=below[:], compare_op=ALU.is_ge, fill=1.0, base=0,
                                                pattern=[[-1, P]], channel_multiplier=1))
                pool.sem_inc(consts, 1)
                pool.wait_ge(filled, 8 * 16)
                def scatter(k):
                    with pool.Fori(0, ET // (2 * G)) as i:
                        for h in range(2):
                            pool.wait_ge(staged, 2 * i + (h + 1 + k * (ET // G)))
                            pool.sem_inc(scattering, 1)
                            for t in range(G):
                                nc.gpsimd.indirect_dma_start(
                                    (pay_a, pay_b)[k], bass.IndirectOffsetOnAxis(ap=pos_st[:, h, t:t + 1], axis=0),
                                    pay_st[:, h, t, :], None).then_inc((out0, out1)[h], 16)
                    pool.wait_ge(out0, (k + 1) * 16 * ET // 2)
                    pool.wait_ge(out1, (k + 1) * 16 * ET // 2)

                scatter(0)
                pool.wait_ge(run_known, 1)
                with pool.If(pool.value_load(unsorted[0:1, 0:1], min_val=0, max_val=1)):
                    scatter(1)

            @block.scalar
            def _(act):
                n = ET // (2 * G)

                def stage(k):
                    for h in range(2):
                        if k:
                            act.wait_ge((out0, out1)[h], 16 * G * n)
                        nc.scalar.copy(pos_st[:, h, :], addr[k][:, h * G:(h + 1) * G])
                        nc.scalar.copy(pay_st[:, h], pay[k][:, h * G:(h + 1) * G, :]).then_inc(staged, 1)
                    with act.Fori(1, n) as i:
                        for h in range(2):
                            act.wait_ge((out0, out1)[h], 16 * G * i + 16 * G * n * k)
                            nc.scalar.copy(pos_st[:, h, :], addr[k][:, bass.ds(i * (2 * G) + h * G, G)])
                            nc.scalar.copy(pay_st[:, h], pay[k][:, bass.ds(i * (2 * G) + h * G, G), :]).then_inc(staged, 1)

                act.wait_ge(rank_a, 1)
                stage(0)
                act.wait_ge(rank_b, 1)
                act.wait_ge(run_known, 1)
                with act.If(act.value_load(unsorted[0:1, 0:1], min_val=0, max_val=1)):
                    stage(1)

            @block.tensor
            def _(pe):
                for k in range(2):
                    pe.wait_ge(counted, k + 1)
                    if k == 0:
                        pe.wait_ge(consts, 1)
                    nc.tensor.matmul(ps[:, 0, 0:NBLK], below[:], cnt[:], start=True, stop=True)
                    nc.tensor.matmul(ps[:, 1, 0:NBLK], ones[:], cnt[:], start=True, stop=True).then_inc(prefixed, 1)
                pe.wait_ge(counted_falls, 1)
                nc.tensor.matmul(ps[:, 2, 0:1], ones[:], falls[:], start=True, stop=True).then_inc(fell, 1)

            @block.vector
            def _(dve):
                ch = Chain(dve, dve_chain)
                ch.link(nc.vector.memset(x_sb[:, NB - 1, :], 0.0))
                ch.link(nc.vector.memset(src[:], EMPTY_DST))
                ch.link(nc.vector.memset(dst[:], EMPTY_DST))
                ch.link(nc.vector.memset(after[:], EMPTY_DST))
                dve.sem_inc(made, 1)
                nc.vector.memset(empty[:, :, 0:1], DUMMY)
                nc.vector.memset(empty[:, :, 1:2], 0)
                nc.vector.memset(empty[:, :, 2:3], -1)
                ch.link(nc.vector.memset(empty[:, :, 3:4], EMPTY_DST))
                dve.sem_inc(made, 1)
                ch.link(nc.vector.memset(zero[:], 0.0))
                dve.wait_ge(consts, 1)
                dve.wait_ge(loaded, 128)
                n = ch.n

                def pairs_of_blocks(k, n):
                    ch = Chain(dve, dve_chain, start=n)
                    ch.link(nc.vector.memset(qblk[:], 0.0))
                    n += ch.n
                    with dve.Fori(0, NB) as b:
                        lp = Chain(dve, dve_chain, start=b + n)
                        lp.link(nc.vector.scalar_tensor_tensor(qblk[:], qno[:], cum[0:1, bass.ds(b, 1)], qblk[:], ALU.is_ge, ALU.add))
                    n += NB
                    ch = Chain(dve, dve_chain, start=n)
                    ch.link(nc.vector.tensor_scalar((blk_a, blk_b)[k][:], qblk[:], float(NB - 1), None, ALU.min))
                    return n + ch.n

                def runs_of_list(n):
                    ch = Chain(dve, dve_chain, start=n)
                    ch.link(nc.vector.tensor_scalar(qrun[:], qno[:], float(2 * P), None, ALU.mult))
                    n += ch.n
                    with dve.Fori(0, NB) as b:
                        lp = Chain(dve, dve_chain, start=b * 2 + n)
                        lp.link(nc.vector.tensor_scalar(qstep[:], qno[:], cum[0:1, bass.ds(b, 1)], gain[0:1, bass.ds(b, 1)], ALU.is_ge, ALU.mult))
                        lp.link(nc.vector.tensor_tensor(qrun[:], qrun[:], qstep[:], ALU.add))
                    n += NB * 2
                    ch = Chain(dve, dve_chain, start=n)
                    ch.link(nc.vector.tensor_scalar(qfrom[:], qrun[:], float(E), None, ALU.min))
                    ch.link(nc.vector.tensor_tensor(mask[:], dst[:], after[:], ALU.is_gt))
                    nc.vector.tensor_reduce(falls[:], mask[:], AX.X, ALU.add).then_inc(counted_falls, 1)
                    dve.wait_ge(fell, 1)
                    ch.link(nc.vector.tensor_scalar(unsorted[:], ps[0:1, 2, 0:1], 1.0, None, ALU.min))
                    dve.sem_inc(run_known, 1)
                    return n + ch.n

                for k, (key, other) in enumerate(((src, dst), (dst, src))):
                    ch = Chain(dve, dve_chain, start=n)
                    ch.link(nc.vector.tensor_scalar(addr[k][:], key[:], 7, None, ALU.logical_shift_right))
                    ch.link(nc.vector.tensor_copy(blkf[:], addr[k][:]))
                    ch.link(nc.vector.tensor_scalar(addr[k][:], key[:], P - 1, None, ALU.bitwise_and))
                    nc.vector.tensor_copy(pay[k][:, :, 0:1], other[:].unsqueeze(2))
                    nc.vector.tensor_copy(pay[k][:, :, 1:2], eno[:].unsqueeze(2))
                    nc.vector.tensor_copy(pay[k][:, :, 2:3], addr[k][:].unsqueeze(2))
                    ch.link(nc.vector.tensor_copy(pay[k][:, :, 3:4], key[:].unsqueeze(2)))
                    n += ch.n
                    if k:
                        dve.sem_inc(recorded, 1)
                    with dve.Fori(0, NBLK) as b:
                        lp = Chain(dve, dve_chain, start=b * 2 + n)
                        lp.link(nc.vector.tensor_scalar(mask[:], blkf[:], bno[:, bass.ds(b, 1)], None, ALU.is_equal))
                        lp.link(nc.vector.tensor_reduce(cnt[:, bass.ds(b, 1)], mask[:], AX.X, ALU.add))
                    n += NBLK * 2
                    dve.sem_inc(counted, 1)
                    dve.wait_ge(prefixed, k + 1)
                    ch = Chain(dve, dve_chain, start=n)
                    ch.link(nc.vector.tensor_scalar(pairs_i[:], ps[:, 1, 0:NBLK], float(2 * P - 1), None, ALU.add))
                    ch.link(nc.vector.tensor_scalar(pairs_i[:], pairs_i[:], 8, None, ALU.logical_shift_right))
                    ch.link(nc.vector.tensor_copy(pairs_f[:], pairs_i[:]))
                    ch.link(nc.vector.tensor_tensor_scan(cum[:], pairs_f[:], zero[:], 0.0, ALU.add, ALU.add))
                    ch.link(nc.vector.scalar_tensor_tensor(gain[:], pairs_f[:], float(-2 * P), ps[:, 1, 0:NBLK], ALU.mult, ALU.add))
                    ch.link(nc.vector.tensor_tensor(pairs_f[:], cum[:], pairs_f[:], ALU.subtract))
                    ch.link(nc.vector.memset(pairs_f[:, NB:NBLK], float(NPAIR)))
                    ch.link(nc.vector.scalar_tensor_tensor(off[:], pairs_f[:], float(2 * P), ps[:, 0, 0:NBLK], ALU.mult, ALU.add))
                    n += ch.n
                    if k:
                        n = pairs_of_blocks(k, n)
                        n = runs_of_list(n)
                    ch = Chain(dve, dve_chain, start=n)
                    ch.link(nc.vector.memset(pos[:], 0.0))
                    n += ch.n
                    with dve.Fori(0, NBLK) as b:
                        lp = Chain(dve, dve_chain, start=b * 4 + n)
                        lp.link(nc.vector.tensor_scalar(mask[:], blkf[:], bno[:, bass.ds(b, 1)], None, ALU.is_equal))
                        lp.link(nc.vector.tensor_tensor_scan(scan[:], mask[:], mask[:], off[:, bass.ds(b, 1)], ALU.add, ALU.max))
                        lp.link(nc.vector.tensor_tensor(scan[:], scan[:], mask[:], ALU.mult))
                        lp.link(nc.vector.tensor_tensor(pos[:], pos[:], scan[:], ALU.add))
                    n += NBLK * 4
                    ch = Chain(dve, dve_chain, start=n)
                    si, lo = addr[k], scan[:].bitcast(I32)
                    ch.link(nc.vector.tensor_scalar(si[:], pos[:], -1.0, None, ALU.add))
                    ch.link(nc.vector.tensor_scalar(lo, si[:], P - 1, None, ALU.bitwise_and))
                    ch.link(nc.vector.tensor_scalar(si[:], si[:], 7, None, ALU.logical_shift_right))
                    ch.link(nc.vector.scalar_tensor_tensor(place[:], lo, float(PAYC), si[:], ALU.mult, ALU.add))
                    ch.link(nc.vector.tensor_copy(si[:], place[:]))
                    n += ch.n
                    dve.sem_inc((rank_a, rank_b)[k], 1)
                    if not k:
                        n = pairs_of_blocks(k, n)


def load_order(nc, pay, idx, eid, loc):
    with (nc.sbuf_tensor([P, NTX, 4], I32) as rec, nc.semaphore() as loaded, nc.semaphore() as spread, nc.Block() as block):
        @block.sync
        def _(sp):
            sp.dma_start(rec[:].rearrange("p t c -> p (t c)"), pay.rearrange("(p t) c -> p (t c)", p=P)).then_inc(loaded, 16)

        @block.vector
        def _(dve):
            dve.wait_ge(loaded, 16)
            nc.vector.tensor_copy(idx[:].unsqueeze(2), rec[:, :, 0:1])
            nc.vector.tensor_copy(eid[:].unsqueeze(2), rec[:, :, 1:2])
            nc.vector.tensor_copy(loc[:].unsqueeze(2), rec[:, :, 2:3]).then_inc(spread, 1)
            dve.wait_ge(spread, 1)
            nc.vector.memset(idx[:, NT:NTX], DUMMY)
            nc.vector.memset(eid[:, NT:NTX], 0)
            nc.vector.memset(loc[:, NT:NTX], -1.0).then_inc(spread, 1)
            dve.wait_ge(spread, 2)


def load_order_by_dst(nc, pay, ones, blk, idx, loc, first, fence):
    es = ExitStack()
    sb = lambda shape, dt=F32: es.enter_context(nc.sbuf_tensor(fresh("buf"), shape, dt))
    sem = lambda: es.enter_context(nc.semaphore(fresh("sem")))
    HP = NPAIR // 2
    assert HP <= 512
    with es:
        rec, blkf, pair_blk, place, valid, node = sb([P, NTX, 4], I32), sb([1, NPAIR]), sb([P, NPAIR]), sb([P, NT]), sb([P, NT]), sb([P, NT])
        ps = es.enter_context(nc.psum_tensor(fresh("psum"), [P, 2, 512], F32))
        loaded, floated, spread, dve_chain = (sem() for _ in range(4))
        with nc.Block() as block:
            @block.sync
            def _(sp):
                sp.dma_start(rec[:].rearrange("p t c -> p (t c)"), pay.rearrange("(p t) c -> p (t c)", p=P)).then_inc(loaded, 16)

            @block.tensor
            def _(pe):
                pe.wait_ge(floated, 1)
                for k in range(2):
                    last = nc.tensor.matmul(ps[:, k, 0:HP], ones[0:1, :], blkf[:, k * HP:(k + 1) * HP], start=True, stop=True)
                last.then_inc(spread, 1)

            @block.vector
            def _(dve):
                ch = Chain(dve, dve_chain)
                nc.vector.tensor_copy(blkf[:], blk[:, 0:NPAIR]).then_inc(floated, 1)
                dve.wait_ge(loaded, 16)
                ch.link(nc.vector.tensor_copy(place[:].unsqueeze(2), rec[:, 0:NT, 3:4]))
                dve.wait_ge(spread, 1)
                ch.link(nc.vector.memset(first, 1.0))
                for k in range(2):
                    ch.link(nc.vector.tensor_copy(pair_blk[:, k * HP:(k + 1) * HP], ps[:, k, 0:HP]))
                ch.link(nc.vector.tensor_tensor(first[:, 1:NPAIR], pair_blk[:, 1:NPAIR], pair_blk[:, 0:NPAIR - 1], ALU.not_equal))
                ch.link(nc.vector.memset(first[:, 0:NPAIR].rearrange("p (n q) -> p n q", q=PAIRS)[:, :, 0:1], 1.0))
                ch.link(nc.vector.tensor_scalar(fence, first, -3.0e38, None, ALU.mult))
                for k in range(2):
                    part = place[:, k * 2 * HP:(k + 1) * 2 * HP].rearrange("p (q s) -> p q s", s=2)
                    ch.link(nc.vector.scalar_tensor_tensor(part, bc(ps[:, k, 0:HP].unsqueeze(2), [P, HP, 2]), float(-P), part, ALU.mult, ALU.add))
                ch.link(nc.vector.tensor_scalar(valid[:], place[:], 0.0, None, ALU.is_ge))
                ch.link(nc.vector.scalar_tensor_tensor(valid[:], place[:], float(P), valid[:], ALU.is_lt, ALU.mult))
                ch.link(nc.vector.scalar_tensor_tensor(place[:], place[:], 1.0, valid[:], ALU.add, ALU.mult))
                ch.link(nc.vector.tensor_scalar(loc[:, 0:NT], place[:], -1.0, None, ALU.add))
                ch.link(nc.vector.tensor_copy(node[:].unsqueeze(2), rec[:, 0:NT, 0:1]))
                ch.link(nc.vector.scalar_tensor_tensor(node[:], node[:], float(-DUMMY), valid[:], ALU.add, ALU.mult))
                ch.link(nc.vector.tensor_scalar(idx[:, 0:NT], node[:], float(DUMMY), None, ALU.add))
                nc.vector.memset(idx[:, NT:NTX], DUMMY)
                ch.link(nc.vector.memset(loc[:, NT:NTX], -1.0))


KB = 7
assert NB % KB == 0


def ln_stats(ch, act, src, tmp, st):
    sh = [P, NB, D]
    ch.link(nc_v(ch).tensor_reduce(st["mean"][:], src, AX.X, ALU.add))
    ch.link(nc_v(ch).tensor_scalar(st["mean"][:], st["mean"][:], 1.0 / D, None, ALU.mult))
    ch.link(nc_v(ch).tensor_tensor(tmp[:], src, bc(st["mean"][:].unsqueeze(2), sh), ALU.subtract))
    ch.link(nc_v(ch).tensor_tensor(tmp[:], tmp[:], tmp[:], ALU.mult))
    ch.link(nc_v(ch).tensor_reduce(st["var"][:], tmp[:], AX.X, ALU.add))
    nc_v(ch).tensor_scalar(st["var"][:], st["var"][:], 1.0 / D, LN_EPS, ALU.mult, ALU.add).then_inc(st["var_ready"], 1)
    st["n"] += 1
    ch.eng.wait_ge(st["sd_ready"], st["n"])
    ch.link(nc_v(ch).reciprocal(st["rstd"][:], st["sd"][:]))
    ch.link(nc_v(ch).scalar_tensor_tensor(st["nmr"][:], st["mean"][:], -1.0, st["rstd"][:], ALU.mult, ALU.mult))


def nc_v(ch):
    return ch.eng.bass.vector


def ln_sqrt(nc, act, st, n):
    act.wait_ge(st["var_ready"], n)
    nc.scalar.activation(st["sd"][:], st["var"][:], ACT.Sqrt).then_inc(st["sd_ready"], 1)


def ln_buffers(sb, sem):
    return dict(mean=sb([P, NB]), var=sb([P, NB]), sd=sb([P, NB]), rstd=sb([P, NB]), nmr=sb([P, NB]),
                var_ready=sem(), sd_ready=sem(), n=0)


def mm_buffers(es, nc, sb, sem, j):
    return dict(stage=sb([P, KB, j, P]), hT=sb([P, j, P]), psT=es.enter_context(nc.psum_tensor(fresh("psum"), [P, j, 512], F32)),
                psO=es.enter_context(nc.psum_tensor(fresh("psum"), [P, 512], F32)), staged=sem(), transposed=sem(), turned=sem(),
                produced=sem(), consumed=sem(), j=j)


def mm_scalar(act, m, fill):
    with act.Fori(0, NB // KB) as i:
        for k in range(KB):
            act.wait_ge(m["transposed"], i * KB + (k + 1))
            fill(k, i * KB + k, m["stage"][:, k]).then_inc(m["staged"], 1)


def mm_tensor(nc, pe, m, ident, weights):
    pe.sem_inc(m["transposed"], KB)
    with pe.Fori(0, NB // KB) as i:
        for k in range(KB):
            pe.wait_ge(m["staged"], i * KB + (k + 1))
            for j in range(m["j"]):
                t = nc.tensor.transpose(m["psT"][:, j, 0:P], m["stage"][:, k, j, :], ident[:])
            t.then_inc(m["transposed"], 1)
            pe.wait_ge(m["turned"], i * KB + (k + 1))
            for j in range(m["j"]):
                t = nc.tensor.matmul(m["psO"][:, 0:D], m["hT"][:, j, :], weights[j], start=(j == 0), stop=(j == m["j"] - 1))
            t.then_inc(m["produced"], 1)


def mm_vector(nc, dve, m, use):
    with dve.Fori(0, NB // KB) as i:
        for k in range(KB):
            dve.wait_ge(m["transposed"], i * KB + (k + 1 + KB))
            nc.vector.tensor_copy(m["hT"][:], m["psT"][:, :, 0:P]).then_inc(m["turned"], 1)
            dve.wait_ge(m["produced"], i * KB + (k + 1))
            use(i * KB + k, m["psO"][:, 0:D], i, k)


def row_of(v):
    return v.rearrange("(o d) -> o d", o=1)


def l0_nodes(nc, c, ins, a_src):
    es = ExitStack()
    sb = lambda shape, dt=F32: es.enter_context(nc.sbuf_tensor(fresh("buf"), shape, dt))
    sem = lambda: es.enter_context(nc.semaphore(fresh("sem")))
    tab = c["tab"]
    with es:
        tmp, st, m = sb([P, NB, D]), ln_buffers(sb, sem), mm_buffers(es, nc, sb, sem, 1)
        w, wb, aw = sb([D, D]), sb([P, D]), sb([P, 2, D])
        loaded, stats, dve_chain, tabled, stored, scored = (sem() for _ in range(6))
        with nc.Block() as block:
            @block.sync
            def _(sp):
                sp.dma_start(w[:], ins["L0_gnn_W_w"]).then_inc(loaded, 16)
                sp.dma_start(wb[:], row_of(ins["L0_gnn_W_b"]).broadcast_to([P, D])).then_inc(loaded, 16)
                for k in range(2):
                    sp.dma_start(aw[:, k], ins["L0_gnn_a_w"][k * D:(k + 1) * D, :].rearrange("d o -> o d").broadcast_to([P, D])).then_inc(loaded, 16)
                sp.wait_ge(tabled, 1)
                sp.dma_start(c["table"].rearrange("(b p) w -> p b w", p=P), tab[:]).then_inc(stored, 16)
                sp.wait_ge(stored, 16)

            @block.scalar
            def _(act):
                ln_sqrt(nc, act, st, 1)
                act.wait_ge(stats, 1)
                mm_scalar(act, m, lambda k, b, stage: nc.scalar.activation(
                    stage[:, 0, :], flat(c["x"][:, bass.ds(b, 1), :]), ACT.Relu,
                    bias=st["nmr"][:, bass.ds(b, 1)], scale=st["rstd"][:, bass.ds(b, 1)]))

            @block.tensor
            def _(pe):
                pe.wait_ge(loaded, 64)
                mm_tensor(nc, pe, m, c["ident"], [w[:]])

            @block.vector
            def _(dve):
                ch = Chain(dve, dve_chain)
                ln_stats(ch, None, c["x"][:], tmp, st)
                dve.sem_inc(stats, 1)
                ch.link(nc.vector.memset(tab[:], 0.0))
                dve.wait_ge(loaded, 64)
                mm_vector(nc, dve, m, lambda b, ps, i, k: nc.vector.tensor_tensor(
                    flat(tab[:, bass.ds(b, 1), 0:D]), ps, wb[:], ALU.add).then_inc(m["consumed"], 1))
                dve.wait_ge(m["consumed"], NB)
                nc.vector.memset(tab[:, :, D:D + 1], 1.0)
                ch.link(nc.vector.tensor_tensor(tmp[:], tab[:, :, 0:D], bc(aw[:, 0:1], [P, NB, D]), ALU.mult))
                ch.link(nc.vector.tensor_reduce(a_src[:], tmp[:], AX.X, ALU.add))
                ch.link(nc.vector.tensor_tensor(tmp[:], tab[:, :, 0:D], bc(aw[:, 1:2], [P, NB, D]), ALU.mult))
                ch.link(nc.vector.tensor_reduce(tab[:, :, D + 1:D + 2], tmp[:], AX.X, ALU.add))
                dve.sem_inc(tabled, 1)


def half_of(i, h, ahead=0, R=2):
    return i * (R * HALF) + (h + ahead) * HALF


def onehot(nc, c, oh, tile0):
    return nc.vector.tensor_tensor(oh, bc(c["iota"][:].unsqueeze(1), [P, HALF, P]),
                                   bc(c["loc"][:, bass.ds(tile0, HALF)].unsqueeze(2), [P, HALF, P]), ALU.is_equal)


def gather_half(nc, pool, table, stage, rows, sem, used):
    for t in range(HALF):
        nc.gpsimd.indirect_dma_start(rows[:, t, 0:used], None, table, bass.IndirectOffsetOnAxis(ap=stage[:, t:t + 1], axis=0)).then_inc(sem, 16)


def pair_blocks(nc, engine, blk, i, h, ahead=0, R=2):
    return nc.values_load_multi_w_load_instructions(
        blk[0:1, bass.ds(i * (R * PAIRS) + (h + ahead) * PAIRS, PAIRS)], engines=[engine], min_val=0, max_val=NB - 1,
        skip_runtime_bounds_check_because=BLOCK_RANGE)[1]


def sum_pairs(nc, ps, oh, rows, width):
    for q in range(PAIRS):
        for s in range(2):
            last = nc.tensor.matmul(ps[:, q // 3, (q % 3) * W:(q % 3) * W + width], oh[:, 2 * q + s, :], rows[:, 2 * q + s, 0:width],
                                    start=(s == 0), stop=(s == 1))
    return last


def add_pairs(nc, dve, agg, ps, blocks, width, added, i, h, R=2):
    for q in range(PAIRS):
        dve.wait_ge(added, i * (R * PAIRS) + (h * PAIRS + q + 1))
        a = flat(agg[:, bass.ds(blocks[q], 1), 0:width])
        nc.vector.tensor_tensor(a, a, ps[:, q // 3, (q % 3) * W:(q % 3) * W + width], ALU.add).then_inc(added, 1)


def turn_onehot(nc, c, oh, psT, sg):
    for t in range(4):
        last = nc.tensor.transpose(psT[:, sg % 2, t * P:(t + 1) * P], oh[:, 4 * sg + t, :], c["ident"][:])
    return last


def l0_edges(nc, c, ins, blk, a_src):
    es = ExitStack()
    sb = lambda shape, dt=F32: es.enter_context(nc.sbuf_tensor(fresh("buf"), shape, dt))
    sem = PhaseSemaphores(nc)
    es.callback(sem.give_back)
    agg, R = c["agg"], 4
    assert NH % R == 0
    with es:
        stage, rows, oh = sb([P, R, HALF], I32), sb([P, R, HALF, W]), sb([P, 2, HALF, P])
        hot16, ohT = sb([P, 2, HALF, P]), sb([P, 2, 4 * P])
        ab, e1, e2, pen, p = sb([P, 1]), sb([P, HALF]), sb([P, HALF]), sb([P, HALF]), sb([P, 2, HALF])
        mx, m1, mrun, mold, negm, fac = sb([P, 1]), sb([1, 1]), sb([1, 1]), sb([P, 1]), sb([P, 1]), sb([P, 2])
        psT = es.enter_context(nc.psum_tensor(fresh("psum"), [P, 2, 512], F32))
        psE = es.enter_context(nc.psum_tensor(fresh("psum"), [P, 512], F32))
        psM = es.enter_context(nc.psum_tensor(fresh("psum"), [P, 2, 512], F32))
        psA = es.enter_context(nc.psum_tensor(fresh("psum"), [P, 3, 512], F32))
        (loaded, staged, got0, got1, got2, got3, gathering, hot, ohT_ps, ohT_ready, expanded, maxed, max_turned, max_run, max_spread, newmax,
         weights, weighted, summed, scaled, added, dve_chain) = (sem() for _ in range(22))
        got = (got0, got1, got2, got3)
        DV = 6
        with nc.Block() as block:
            @block.sync
            def _(sp):
                sp.dma_start(ab[:], row_of(ins["L0_gnn_a_b"]).broadcast_to([P, 1])).then_inc(loaded, 16)
                sp.wait_ge(loaded, 16)

            @block.gpsimd
            def _(pool):
                def fetch(n, s):
                    pool.wait_ge(staged, n + 1)
                    pool.sem_inc(gathering, 1)
                    gather_half(nc, pool, c["table"], stage[:, s], rows[:, s], got[s], W)
                fetch(0, 0)
                with pool.Fori(0, NH // R) as i:
                    for h in range(R):
                        fetch(R * i + (h + 1), (h + 1) % R)

            @block.scalar
            def _(act):
                def copies(n):
                    for sg in range(4):
                        act.wait_ge(ohT_ps, 4 * n + (sg + 1))
                        if sg >= 2:
                            act.wait_ge(expanded, 4 * n + (sg - 1))
                        nc.scalar.copy(ohT[:, sg % 2, :], psT[:, sg % 2, :]).then_inc(ohT_ready, 1)

                def weigh(n, h):
                    act.wait_ge(newmax, n + 1)
                    nc.scalar.activation(p[:, h, :], e2[:], ACT.Exp, bias=negm[:])
                    nc.scalar.activation(fac[:, h:h + 1], mold[:], ACT.Exp, bias=negm[:]).then_inc(weights, 1)

                for s in range(R):
                    nc.scalar.copy(stage[:, s, :], c["idx"][:, s * HALF:(s + 1) * HALF]).then_inc(staged, 1)
                copies(0)
                weigh(0, 0)
                with act.Fori(0, NH // R) as i:
                    for h in range(R):
                        copies(R * i + (h + 1))
                        act.wait_ge(added, i * (R * PAIRS) + (h * PAIRS + 1))
                        act.wait_ge(weights, R * i + (h + 1))
                        nc.scalar.activation(flat(agg[:]), flat(agg[:]), ACT.Copy, scale=fac[:, h % 2:h % 2 + 1]).then_inc(scaled, 1)
                        weigh(R * i + (h + 1), (h + 1) % 2)
                        act.wait_ge(summed, R * i + (h + 1))
                        nc.scalar.copy(stage[:, h, :], c["idx"][:, bass.ds(half_of(i, h, R, R), HALF)]).then_inc(staged, 1)

            @block.tensor
            def _(pe):
                def spread(n, h, blocks):
                    pe.wait_ge(hot, n + 1)
                    for sg in range(4):
                        if sg >= 2:
                            pe.wait_ge(ohT_ready, 4 * n + (sg - 1))
                        turn_onehot(nc, c, hot16[:, h], psT, sg).then_inc(ohT_ps, 1)
                        if sg >= 1:
                            expand(n, sg - 1, blocks)
                    expand(n, 3, blocks)

                def maximum(n):
                    pe.wait_ge(maxed, n + 1)
                    nc.tensor.transpose(psM[0:1, 0, 0:P], mx[:], c["ident"][:]).then_inc(max_turned, 1)
                    pe.wait_ge(max_run, n + 1)
                    nc.tensor.matmul(psM[:, 1, 0:1], c["ones"][0:1, :], mrun[:], start=True, stop=True).then_inc(max_spread, 1)

                def expand(n, sg, blocks):
                    pe.wait_ge(ohT_ready, 4 * n + (sg + 1))
                    for t in range(4):
                        last = nc.tensor.matmul(psE[:, 4 * sg + t:4 * sg + t + 1], ohT[:, sg % 2, t * P:(t + 1) * P],
                                                flat(a_src[:, bass.ds(blocks[(4 * sg + t) // 2], 1), :]), start=True, stop=True)
                    last.then_inc(expanded, 1)

                b0 = nc.values_load_multi_w_load_instructions(blk[0:1, 0:PAIRS], engines=[ENG.PE], min_val=0, max_val=NB - 1,
                                                              skip_runtime_bounds_check_because=BLOCK_RANGE)[1]
                spread(0, 0, b0)
                maximum(0)
                with pe.Fori(0, NH // R) as i:
                    for h in range(R):
                        blocks = pair_blocks(nc, ENG.PE, blk, i, h, 1, R)
                        spread(R * i + (h + 1), (h + 1) % 2, blocks)
                        maximum(R * i + (h + 1))
                        pe.wait_ge(weighted, R * i + (h + 1))
                        pe.wait_ge(got[h], 256 * i + 256)
                        pe.wait_ge(added, i * (R * PAIRS) + (h * PAIRS + 1))
                        sum_pairs(nc, psA, oh[:, h % 2], rows[:, h], D + 1).then_inc(summed, 1)

            @block.vector
            def _(dve):
                def scores(n, s, rows_at):
                    lp = Chain(dve, dve_chain, start=n * DV + 1)
                    dve.wait_ge(expanded, 4 * n + 4)
                    dve.wait_ge(got[s], rows_at)
                    ad = rows[:, s, :, D + 1:D + 2].rearrange("p t o -> p (t o)")
                    lp.link(nc.vector.scalar_tensor_tensor(e1[:], psE[:, 0:HALF], ab[:], ad, ALU.add, ALU.add))
                    lp.link(nc.vector.scalar_tensor_tensor(e2[:], e1[:], 0.01, e1[:], ALU.mult, ALU.max))
                    lp.link(nc.vector.tensor_scalar(pen[:], c["loc"][:, bass.ds(n * HALF, HALF)], 0.0, -NEG, ALU.min, ALU.mult))
                    lp.link(nc.vector.tensor_tensor(e2[:], e2[:], pen[:], ALU.add))
                    nc.vector.tensor_reduce(mx[:], e2[:], AX.X, ALU.max).then_inc(maxed, 1)

                def weigh(n, h):
                    lp = Chain(dve, dve_chain, start=n * DV + 5)
                    dve.wait_ge(max_turned, n + 1)
                    lp.link(nc.vector.tensor_reduce(m1[:], psM[0:1, 0, 0:P], AX.X, ALU.max))
                    nc.vector.tensor_tensor(mrun[:], mrun[:], m1[:], ALU.max).then_inc(max_run, 1)
                    dve.wait_ge(max_spread, n + 1)
                    lp.link(nc.vector.tensor_scalar(mold[:], negm[:], -1.0, None, ALU.mult))
                    nc.vector.tensor_scalar(negm[:], psM[:, 1, 0:1], -1.0, None, ALU.mult).then_inc(newmax, 1)
                    dve.wait_ge(weights, n + 1)
                    nc.vector.tensor_tensor(oh[:, h], hot16[:, h], bc(p[:, h, :].unsqueeze(2), [P, HALF, P]), ALU.mult).then_inc(weighted, 1)
                    assert lp.n == DV - 4

                nc.vector.memset(mrun[:], NEG)
                nc.vector.memset(negm[:], -NEG).then_inc(dve_chain, 1)
                nc.vector.memset(agg[:], 0.0).then_inc(added, 1)
                dve.wait_ge(loaded, 16)
                dve.wait_ge(dve_chain, 1)
                onehot(nc, c, hot16[:, 0], 0).then_inc(hot, 1)
                onehot(nc, c, hot16[:, 1], HALF).then_inc(hot, 1)
                scores(0, 0, 256)
                weigh(0, 0)
                with dve.Fori(0, NH // R) as i:
                    for h in range(R):
                        scores(R * i + (h + 1), (h + 1) % R, 256 * i + 256 * ((h + 1) // R + 1))
                        onehot(nc, c, hot16[:, h % 2], half_of(i, h, 2, R)).then_inc(hot, 1)
                        blocks = pair_blocks(nc, ENG.DVE, blk, i, h, 0, R)
                        weigh(R * i + (h + 1), (h + 1) % 2)
                        dve.wait_ge(summed, R * i + (h + 1))
                        dve.wait_ge(scaled, R * i + (h + 1))
                        add_pairs(nc, dve, agg, psA, blocks, D + 1, added, i, h, R)


def l0_finish(nc, c):
    agg, x = c["agg"], c["x"]
    es = ExitStack()
    sb = lambda shape, dt=F32: es.enter_context(nc.sbuf_tensor(fresh("buf"), shape, dt))
    sem = lambda: es.enter_context(nc.semaphore(fresh("sem")))
    with es:
        z, zi = sb([P, 1]), sb([P, 1])
        ps = es.enter_context(nc.psum_tensor(fresh("psum"), [P, 512], F32))
        dve_chain, zed, total = sem(), sem(), sem()
        with nc.Block() as block:
            @block.tensor
            def _(pe):
                pe.wait_ge(zed, 1)
                nc.tensor.matmul(ps[:, 0:1], c["ones"][:], z[:], start=True, stop=True).then_inc(total, 1)

            @block.vector
            def _(dve):
                ch = Chain(dve, dve_chain)
                nc.vector.tensor_reduce(z[:], agg[:, :, D:D + 1], AX.XY, ALU.add).then_inc(zed, 1)
                dve.wait_ge(total, 1)
                ch.link(nc.vector.reciprocal(zi[:], ps[:, 0:1]))
                ch.link(nc.vector.scalar_tensor_tensor(x[:], agg[:, :, 0:D], zi[:], x[:], ALU.mult, ALU.add))


def store_phase(nc, x_sb, out):
    with nc.semaphore() as stored, nc.Block() as block:
        @block.sync
        def _(sp):
            sp.dma_start(out[0:(NB - 1) * P, :].rearrange("(b p) d -> p b d", p=P), x_sb[:, 0:NB - 1, :]).then_inc(stored, 16)
            sp.dma_start(out[(NB - 1) * P:N, :], x_sb[0:LAST, NB - 1, :]).then_inc(stored, 16)
            sp.wait_ge(stored, 32)


def norm_nodes(ch, nc, st, src, dst):
    sh = [P, NB, D]
    ch.link(nc.vector.tensor_tensor(dst, src, bc(st["rstd"][:].unsqueeze(2), sh), ALU.mult))
    ch.link(nc.vector.tensor_tensor(dst, dst, bc(st["nmr"][:].unsqueeze(2), sh), ALU.add))


def l1_nodes(nc, c, ins, table1):
    es = ExitStack()
    sb = lambda shape, dt=F32: es.enter_context(nc.sbuf_tensor(fresh("buf"), shape, dt))
    sem = lambda: es.enter_context(nc.semaphore(fresh("sem")))
    f = c["tab"][:, :, 0:D]
    with es:
        tmp, st, gb = sb([P, NB, D]), ln_buffers(sb, sem), sb([P, 2, D])
        loaded, dve_chain, tabled, stored = (sem() for _ in range(4))
        with nc.Block() as block:
            @block.sync
            def _(sp):
                sp.dma_start(gb[:, 0], row_of(ins["L1_gnn_ln_gamma"]).broadcast_to([P, D])).then_inc(loaded, 16)
                sp.dma_start(gb[:, 1], row_of(ins["L1_gnn_ln_beta"]).broadcast_to([P, D])).then_inc(loaded, 16)
                sp.wait_ge(tabled, 1)
                sp.dma_start(table1.rearrange("(b p) d -> p b d", p=P), f).then_inc(stored, 16)
                sp.wait_ge(stored, 16)

            @block.scalar
            def _(act):
                ln_sqrt(nc, act, st, 1)
                ln_sqrt(nc, act, st, 2)

            @block.vector
            def _(dve):
                ch = Chain(dve, dve_chain)
                ln_stats(ch, None, c["x"][:], tmp, st)
                norm_nodes(ch, nc, st, c["x"][:], f)
                ch.link(nc.vector.tensor_scalar(f, f, 0.0, None, ALU.max))
                ln_stats(ch, None, f, tmp, st)
                norm_nodes(ch, nc, st, f, f)
                dve.wait_ge(loaded, 32)
                ch.link(nc.vector.tensor_tensor(f, f, bc(gb[:, 0:1], [P, NB, D]), ALU.mult))
                ch.link(nc.vector.tensor_tensor(f, f, bc(gb[:, 1:2], [P, NB, D]), ALU.add))
                dve.sem_inc(tabled, 1)


def l1_edges(nc, c, ins, blk, table1):
    es = ExitStack()
    sb = lambda shape, dt=F32: es.enter_context(nc.sbuf_tensor(fresh("buf"), shape, dt))
    sem = PhaseSemaphores(nc)
    es.callback(sem.give_back)
    agg, tab, edges = c["agg"], c["tab"], ins["edge_attr_128"]
    G = 4 * P
    with es:
        stage, xn, ea, oh = sb([P, 2, 2, HALF], I32), sb([P, 2, HALF, D]), sb([P, 2, HALF, D]), sb([P, 2, HALF, P])
        ohT, s, sT, hS, msg = sb([P, 2, G]), sb([P, 2, G]), sb([P, 4, G]), sb([P, 2, G]), sb([P, 2, G])
        w1, w2, b1, b2 = sb([D, P]), sb([P, D]), sb([P, 1]), sb([P, D])
        psH = es.enter_context(nc.psum_tensor(fresh("psum"), [P, 2, 512], F32))
        psX = es.enter_context(nc.psum_tensor(fresh("psum"), [P, 2, 512], F32))
        psS = es.enter_context(nc.psum_tensor(fresh("psum"), [P, 2, 512], F32))
        psA = es.enter_context(nc.psum_tensor(fresh("psum"), [P, 2, 512], F32))
        (loaded, staged, got0, got1, gathering, hot, ohT_ps, ohT_ready, expanded, partial, s_ready, s_act, sT_ps, sT_ready, h_ps,
         h_ready, theta_ps, biased, msg_ready, summed, added) = (sem() for _ in range(21))
        got = (got0, got1)
        with nc.Block() as block:
            @block.sync
            def _(sp):
                sp.dma_start(w1[:], ins["L1_gnn_phi_w1"]).then_inc(loaded, 16)
                sp.dma_start(w2[:], ins["L1_gnn_phi_w2"]).then_inc(loaded, 16)
                sp.dma_start(b1[:], ins["L1_gnn_phi_b1"].rearrange("(p o) -> p o", o=1)).then_inc(loaded, 16)
                sp.dma_start(b2[:], row_of(ins["L1_gnn_phi_b2"]).broadcast_to([P, D])).then_inc(loaded, 16)
                sp.wait_ge(loaded, 64)

            @block.gpsimd
            def _(pool):
                with pool.Fori(0, NH // 2) as i:
                    for h in range(2):
                        pool.wait_ge(staged, 2 * i + (h + 1))
                        pool.sem_inc(gathering, 1)
                        gather_half(nc, pool, edges, stage[:, h, 1], ea[:, h], got[h], D)
                        gather_half(nc, pool, table1, stage[:, h, 0], xn[:, h], got[h], D)

            @block.scalar
            def _(act):
                act.wait_ge(loaded, 64)
                for h in range(2):
                    nc.scalar.copy(stage[:, h, 0], c["idx"][:, h * HALF:(h + 1) * HALF])
                    nc.scalar.copy(stage[:, h, 1], c["eid"][:, h * HALF:(h + 1) * HALF]).then_inc(staged, 1)
                with act.Fori(0, NH // 2) as i:
                    for h in range(2):
                        n4 = 8 * i + 4 * h
                        for g in range(4):
                            act.wait_ge(ohT_ps, 8 * i + (4 * h + g + 1))
                            if g >= 2:
                                act.wait_ge(expanded, 8 * i + (4 * h + g - 1))
                            nc.scalar.copy(ohT[:, g % 2], psH[:, g % 2]).then_inc(ohT_ready, 1)
                        for g in range(4):
                            act.wait_ge(s_ready, 8 * i + (4 * h + g + 1))
                            nc.scalar.activation(s[:, g % 2], s[:, g % 2], ACT.Silu).then_inc(s_act, 1)
                        for g in range(4):
                            act.wait_ge(sT_ps, 8 * i + (4 * h + g + 1))
                            nc.scalar.copy(sT[:, g], psS[:, g % 2]).then_inc(sT_ready, 1)
                        for g in range(4):
                            act.wait_ge(h_ps, 8 * i + (4 * h + g + 1))
                            if g >= 2:
                                act.wait_ge(theta_ps, 8 * i + (4 * h + g - 1))
                            nc.scalar.activation(hS[:, g % 2], psH[:, g % 2], ACT.Silu, bias=b1[:]).then_inc(h_ready, 1)
                        act.wait_ge(msg_ready, 8 * i + (4 * h + 4))
                        nc.scalar.copy(stage[:, h, 0], c["idx"][:, bass.ds(half_of(i, h, 2), HALF)])
                        nc.scalar.copy(stage[:, h, 1], c["eid"][:, bass.ds(half_of(i, h, 2), HALF)]).then_inc(staged, 1)

            @block.tensor
            def _(pe):
                pe.wait_ge(loaded, 64)
                with pe.Fori(0, NH // 2) as i:
                    for h in range(2):
                        at = lambda g: 8 * i + (4 * h + g + 1)
                        blocks = pair_blocks(nc, ENG.PE, blk, i, h)

                        def expand(g):
                            pe.wait_ge(ohT_ready, at(g))
                            if g >= 2:
                                pe.wait_ge(s_ready, at(g - 2))
                            for t in range(4):
                                last = nc.tensor.matmul(psX[:, g % 2, t * P:(t + 1) * P], ohT[:, g % 2, t * P:(t + 1) * P],
                                                        flat(tab[:, bass.ds(blocks[(4 * g + t) // 2], 1), 0:D]), start=True, stop=True)
                            last.then_inc(expanded, 1)

                        def hidden(g):
                            pe.wait_ge(sT_ready, at(g))
                            nc.tensor.matmul(psH[:, g % 2], w1[:], sT[:, g], start=True, stop=True).then_inc(h_ps, 1)

                        def theta(g):
                            pe.wait_ge(h_ready, at(g))
                            for t in range(4):
                                last = nc.tensor.matmul(psX[:, g % 2, t * P:(t + 1) * P], hS[:, g % 2, t * P:(t + 1) * P], w2[:],
                                                        start=True, stop=True)
                            last.then_inc(theta_ps, 1)

                        def total(g):
                            pe.wait_ge(msg_ready, at(g))
                            if g >= 2:
                                pe.wait_ge(added, i * (2 * PAIRS) + (h * PAIRS + 2 * (g - 1) + 1))
                            for q in range(2):
                                for k in range(2):
                                    last = nc.tensor.matmul(psA[:, g % 2, q * P:(q + 1) * P], oh[:, h, 4 * g + 2 * q + k, :],
                                                            msg[:, g % 2, (2 * q + k) * P:(2 * q + k + 1) * P], start=(k == 0), stop=(k == 1))
                            last.then_inc(summed, 1)

                        pe.wait_ge(hot, 2 * i + (h + 1))
                        for g in range(4):
                            if g >= 2:
                                pe.wait_ge(ohT_ready, at(g - 2))
                            turn_onehot(nc, c, oh[:, h], psH, g).then_inc(ohT_ps, 1)
                            if g >= 1:
                                expand(g - 1)
                        expand(3)
                        for g in range(4):
                            pe.wait_ge(s_act, at(g))
                            if g >= 2:
                                pe.wait_ge(sT_ready, at(g - 2))
                            for t in range(4):
                                last = nc.tensor.transpose(psS[:, g % 2, t * P:(t + 1) * P], s[:, g % 2, t * P:(t + 1) * P], c["ident"][:])
                            last.then_inc(sT_ps, 1)
                        hidden(0)
                        hidden(1)
                        theta(0)
                        hidden(2)
                        theta(1)
                        pe.wait_ge(added, i * (2 * PAIRS) + (h * PAIRS + 1))
                        total(0)
                        hidden(3)
                        theta(2)
                        total(1)
                        theta(3)
                        total(2)
                        total(3)

            @block.vector
            def _(dve):
                nc.vector.memset(agg[:], 0.0).then_inc(added, 1)
                dve.wait_ge(loaded, 64)
                onehot(nc, c, oh[:, 0], 0).then_inc(hot, 1)
                with dve.Fori(0, NH // 2) as i:
                    for h in range(2):
                        at = lambda g: 8 * i + (4 * h + g + 1)
                        blocks = pair_blocks(nc, ENG.DVE, blk, i, h)
                        four = lambda b, g: b[:, h, 4 * g:4 * g + 4, :].rearrange("p t d -> p (t d)")

                        def message(g):
                            dve.wait_ge(theta_ps, at(g))
                            m = msg[:, g % 2].rearrange("p (t d) -> p t d", t=4)
                            nc.vector.tensor_tensor(m, psX[:, g % 2].rearrange("p (t d) -> p t d", t=4), bc(b2[:].unsqueeze(1), [P, 4, D]),
                                                    ALU.add).then_inc(biased, 1)
                            dve.wait_ge(biased, at(g))
                            nc.vector.tensor_tensor(msg[:, g % 2], msg[:, g % 2], four(xn, g), ALU.mult).then_inc(msg_ready, 1)

                        def add(g):
                            dve.wait_ge(summed, at(g))
                            for q in range(2):
                                dve.wait_ge(added, i * (2 * PAIRS) + (h * PAIRS + 2 * g + q + 1))
                                a = flat(agg[:, bass.ds(blocks[2 * g + q], 1), 0:D])
                                nc.vector.tensor_tensor(a, a, psA[:, g % 2, q * P:(q + 1) * P], ALU.add).then_inc(added, 1)

                        dve.wait_ge(got[h], 512 * i + 512)
                        for g in range(4):
                            if g >= 2:
                                dve.wait_ge(sT_ps, at(g - 2))
                            nc.vector.tensor_tensor(s[:, g % 2], four(ea, g), four(xn, g), ALU.add).then_inc(partial, 1)
                            dve.wait_ge(partial, at(g))
                            dve.wait_ge(expanded, at(g))
                            nc.vector.tensor_tensor(s[:, g % 2], s[:, g % 2], psX[:, g % 2], ALU.add).then_inc(s_ready, 1)
                        onehot(nc, c, oh[:, 1 - h], half_of(i, h, 1)).then_inc(hot, 1)
                        message(0)
                        message(1)
                        add(0)
                        message(2)
                        add(1)
                        message(3)
                        add(2)
                        add(3)


def l1_finish(nc, c, ins):
    es = ExitStack()
    sb = lambda shape, dt=F32: es.enter_context(nc.sbuf_tensor(fresh("buf"), shape, dt))
    sem = lambda: es.enter_context(nc.semaphore(fresh("sem")))
    tab, agg, x = c["tab"], c["agg"], c["x"]
    with es:
        w, b, r = sb([D, D]), sb([P, D]), sb([P, 2, D])
        m = mm_buffers(es, nc, sb, sem, 1)
        loaded, dve_chain, ready, biased = (sem() for _ in range(4))
        with nc.Block() as block:
            @block.sync
            def _(sp):
                sp.dma_start(w[:], ins["L1_gnn_theta_w"]).then_inc(loaded, 16)
                sp.dma_start(b[:], row_of(ins["L1_gnn_theta_b"]).broadcast_to([P, D])).then_inc(loaded, 16)
                sp.wait_ge(loaded, 32)

            @block.scalar
            def _(act):
                act.wait_ge(ready, 1)
                mm_scalar(act, m, lambda k, bl, stage: nc.scalar.activation(stage[:, 0, :], flat(tab[:, bass.ds(bl, 1), 0:D]), ACT.Silu))

            @block.tensor
            def _(pe):
                pe.wait_ge(loaded, 32)
                mm_tensor(nc, pe, m, c["ident"], [w[:]])

            @block.vector
            def _(dve):
                ch = Chain(dve, dve_chain)
                ch.link(nc.vector.tensor_tensor(tab[:, :, 0:D], tab[:, :, 0:D], agg[:, :, 0:D], ALU.add))
                dve.wait_ge(loaded, 32)
                ch.link(nc.vector.tensor_tensor(x[:], x[:], bc(b[:].unsqueeze(1), [P, NB, D]), ALU.add))
                dve.sem_inc(ready, 1)

                def use(bl, ps, i, k):
                    xb = flat(x[:, bass.ds(bl, 1), :])
                    nc.vector.tensor_tensor(xb, xb, ps, ALU.add).then_inc(m["consumed"], 1)
                mm_vector(nc, dve, m, use)
                dve.wait_ge(m["consumed"], NB)


def l2_nodes(nc, c):
    es = ExitStack()
    sb = lambda shape, dt=F32: es.enter_context(nc.sbuf_tensor(fresh("buf"), shape, dt))
    sem = lambda: es.enter_context(nc.semaphore(fresh("sem")))
    tab = c["tab"]
    f = tab[:, :, 0:D]
    with es:
        tmp, st = sb([P, NB, D]), ln_buffers(sb, sem)
        dve_chain, tabled, stored = (sem() for _ in range(3))
        with nc.Block() as block:
            @block.sync
            def _(sp):
                sp.wait_ge(tabled, 1)
                sp.dma_start(c["table"].rearrange("(b p) w -> p b w", p=P), tab[:]).then_inc(stored, 16)
                sp.wait_ge(stored, 16)

            @block.scalar
            def _(act):
                ln_sqrt(nc, act, st, 1)

            @block.vector
            def _(dve):
                ch = Chain(dve, dve_chain)
                ln_stats(ch, None, c["x"][:], tmp, st)
                ch.link(nc.vector.memset(tab[:, :, D:W], 1.0))
                norm_nodes(ch, nc, st, c["x"][:], f)
                ch.link(nc.vector.tensor_scalar(f, f, 0.0, None, ALU.max))
                dve.sem_inc(tabled, 1)


def l2_edges(nc, c, blk):
    es = ExitStack()
    sb = lambda shape, dt=F32: es.enter_context(nc.sbuf_tensor(fresh("buf"), shape, dt))
    sem = lambda: es.enter_context(nc.semaphore(fresh("sem")))
    agg = c["agg"]
    with es:
        stage, rows, oh = sb([P, 2, HALF], I32), sb([P, 2, HALF, W]), sb([P, 2, HALF, P])
        psA = es.enter_context(nc.psum_tensor(fresh("psum"), [P, 2, 3, 512], F32))
        staged, got0, got1, gathering, hot, summed, added = (sem() for _ in range(7))
        got = (got0, got1)
        with nc.Block() as block:
            @block.gpsimd
            def _(pool):
                with pool.Fori(0, NH // 2) as i:
                    for h in range(2):
                        pool.wait_ge(staged, 2 * i + (h + 1))
                        pool.sem_inc(gathering, 1)
                        gather_half(nc, pool, c["table"], stage[:, h], rows[:, h], got[h], W)

            @block.scalar
            def _(act):
                for h in range(2):
                    nc.scalar.copy(stage[:, h], c["idx"][:, h * HALF:(h + 1) * HALF]).then_inc(staged, 1)
                with act.Fori(0, NH // 2) as i:
                    for h in range(2):
                        act.wait_ge(summed, 2 * i + (h + 1))
                        nc.scalar.copy(stage[:, h], c["idx"][:, bass.ds(half_of(i, h, 2), HALF)]).then_inc(staged, 1)

            @block.tensor
            def _(pe):
                with pe.Fori(0, NH // 2) as i:
                    for h in range(2):
                        pe.wait_ge(hot, 2 * i + (h + 1))
                        pe.wait_ge(got[h], 256 * i + 256)
                        sum_pairs(nc, psA[:, h], oh[:, h], rows[:, h], D + 1).then_inc(summed, 1)

            @block.vector
            def _(dve):
                nc.vector.memset(agg[:], 0.0).then_inc(added, 1)
                onehot(nc, c, oh[:, 0], 0).then_inc(hot, 1)
                with dve.Fori(0, NH // 2) as i:
                    for h in range(2):
                        dve.wait_ge(added, i * (2 * PAIRS) + (h * PAIRS + 1))
                        onehot(nc, c, oh[:, 1 - h], half_of(i, h, 1)).then_inc(hot, 1)
                        blocks = pair_blocks(nc, ENG.DVE, blk, i, h)
                        dve.wait_ge(summed, 2 * i + (h + 1))
                        add_pairs(nc, dve, agg, psA[:, h], blocks, D + 1, added, i, h)


def l2_finish(nc, c, ins):
    es = ExitStack()
    sb = lambda shape, dt=F32: es.enter_context(nc.sbuf_tensor(fresh("buf"), shape, dt))
    sem = lambda: es.enter_context(nc.semaphore(fresh("sem")))
    tab, agg, x = c["tab"], c["agg"], c["x"]
    o, mean = tab[:, :, 0:D], agg[:, :, 0:D]
    sh = [P, NB, D]
    with es:
        wl, wr, bl, br = sb([D, D]), sb([D, D]), sb([P, D]), sb([P, D])
        deg, sq, nrm = sb([P, NB]), sb([P, NB]), sb([P, NB])
        m = mm_buffers(es, nc, sb, sem, 2)
        loaded, dve_chain, ready, squared, rooted = (sem() for _ in range(5))
        with nc.Block() as block:
            @block.sync
            def _(sp):
                for d, s in ((wl, ins["L2_gnn_Wl"]), (wr, ins["L2_gnn_Wr"]), (bl, row_of(ins["L2_gnn_bl"]).broadcast_to([P, D])),
                             (br, row_of(ins["L2_gnn_br"]).broadcast_to([P, D]))):
                    sp.dma_start(d[:], s).then_inc(loaded, 16)
                sp.wait_ge(loaded, 64)

            @block.scalar
            def _(act):
                act.wait_ge(ready, 1)

                def fill(k, b, stage):
                    nc.scalar.copy(stage[:, 0, :], flat(tab[:, bass.ds(b, 1), 0:D]))
                    return nc.scalar.copy(stage[:, 1, :], flat(agg[:, bass.ds(b, 1), 0:D]))
                mm_scalar(act, m, fill)
                act.wait_ge(squared, 1)
                nc.scalar.activation(nrm[:], sq[:], ACT.Sqrt).then_inc(rooted, 1)

            @block.tensor
            def _(pe):
                pe.wait_ge(loaded, 64)
                mm_tensor(nc, pe, m, c["ident"], [wl[:], wr[:]])

            @block.vector
            def _(dve):
                ch = Chain(dve, dve_chain)
                ch.link(nc.vector.tensor_scalar(deg[:].unsqueeze(2), agg[:, :, D:D + 1], 1.0, None, ALU.max))
                ch.link(nc.vector.reciprocal(deg[:], deg[:]))
                ch.link(nc.vector.tensor_tensor(mean, mean, bc(deg[:].unsqueeze(2), sh), ALU.mult))
                dve.wait_ge(loaded, 64)
                ch.link(nc.vector.tensor_tensor(bl[:], bl[:], br[:], ALU.add))
                dve.sem_inc(ready, 1)

                def use(b, ps, i, k):
                    nc.vector.tensor_tensor(flat(tab[:, bass.ds(b, 1), 0:D]), ps, bl[:], ALU.add).then_inc(m["consumed"], 1)
                mm_vector(nc, dve, m, use)
                dve.wait_ge(m["consumed"], NB)
                ch.link(nc.vector.tensor_scalar(o, o, 0.0, None, ALU.max))
                ch.link(nc.vector.tensor_tensor(mean, o, o, ALU.mult))
                nc.vector.tensor_reduce(sq[:], mean, AX.X, ALU.add).then_inc(squared, 1)
                dve.wait_ge(rooted, 1)
                ch.link(nc.vector.tensor_scalar(nrm[:], nrm[:], 1e-6, None, ALU.add))
                ch.link(nc.vector.reciprocal(nrm[:], nrm[:]))
                ch.link(nc.vector.tensor_tensor(o, o, bc(nrm[:].unsqueeze(2), sh), ALU.mult))
                ch.link(nc.vector.tensor_tensor(x[:], x[:], o, ALU.add))


SLOPE = 0.2


HW = HEAD_DIM + 1
assert HEADS * HW == W


def heads(ap):
    return ap.rearrange("p t (h k) -> p t h k", h=HEADS)


def features(rows):
    return heads(rows)[:, :, :, 0:HEAD_DIM]


def scores_of(rows):
    return heads(rows)[:, :, :, HEAD_DIM:HW].rearrange("p t h o -> p t (h o)")


def l3_nodes(nc, c, ins, seg):
    es = ExitStack()
    sb = lambda shape, dt=F32: es.enter_context(nc.sbuf_tensor(fresh("buf"), shape, dt))
    sem = lambda: es.enter_context(nc.semaphore(fresh("sem")))
    tab = c["tab"]
    with es:
        tmp, st, m = sb([P, NB, D]), ln_buffers(sb, sem), mm_buffers(es, nc, sb, sem, 1)
        w, wT, att, low = sb([D, D]), sb([D, D]), sb([P, 2, D]), sb([1, W])
        psW = es.enter_context(nc.psum_tensor(fresh("psum"), [P, 512], F32))
        loaded, stats, dve_chain, tabled, stored, w_turned, w_ready = (sem() for _ in range(7))
        with nc.Block() as block:
            @block.sync
            def _(sp):
                sp.dma_start(w[:], ins["L3_gnn_W"]).then_inc(loaded, 16)
                for k, name in enumerate(("L3_gnn_att_src", "L3_gnn_att_dst")):
                    sp.dma_start(att[:, k], ins[name].rearrange("o h k -> o (h k)").broadcast_to([P, D])).then_inc(loaded, 16)
                sp.wait_ge(tabled, 1)
                sp.dma_start(c["table"].rearrange("(b p) w -> p b w", p=P), tab[:]).then_inc(stored, 16)
                sp.wait_ge(stored, 16)
                sp.dma_start(c["table"][DUMMY:DUMMY + 1, :], low[:]).then_inc(stored, 16)
                sp.wait_ge(stored, 32)

            @block.scalar
            def _(act):
                ln_sqrt(nc, act, st, 1)
                act.wait_ge(stats, 1)
                mm_scalar(act, m, lambda k, b, stage: nc.scalar.activation(
                    stage[:, 0, :], flat(c["x"][:, bass.ds(b, 1), :]), ACT.Relu,
                    bias=st["nmr"][:, bass.ds(b, 1)], scale=st["rstd"][:, bass.ds(b, 1)]))

            @block.tensor
            def _(pe):
                pe.wait_ge(loaded, 48)
                nc.tensor.transpose(psW[:, 0:D], w[:], c["ident"][:]).then_inc(w_turned, 1)
                pe.wait_ge(w_ready, 1)
                mm_tensor(nc, pe, m, c["ident"], [wT[:]])

            @block.vector
            def _(dve):
                ch = Chain(dve, dve_chain)
                ch.link(nc.vector.memset(low[:], 0.0))
                ch.link(nc.vector.memset(low[:].rearrange("o (h k) -> o h k", h=HEADS)[:, :, HEAD_DIM:HW], NEG))
                dve.wait_ge(w_turned, 1)
                nc.vector.tensor_copy(wT[:], psW[:, 0:D]).then_inc(w_ready, 1)
                ln_stats(ch, None, c["x"][:], tmp, st)
                dve.sem_inc(stats, 1)
                dve.wait_ge(loaded, 48)
                mm_vector(nc, dve, m, lambda b, ps, i, k: nc.vector.tensor_copy(
                    tab[:, bass.ds(b, 1), :].rearrange("p b (h k) -> p (b h) k", h=HEADS)[:, :, 0:HEAD_DIM],
                    ps.rearrange("p (h k) -> p h k", h=HEADS)).then_inc(m["consumed"], 1))
                dve.wait_ge(m["consumed"], NB)
                for k, score in enumerate((scores_of(tab[:]), seg[:, :, 0:HEADS])):
                    ch.link(nc.vector.tensor_tensor(heads(tmp[:]), features(tab[:]), bc(heads(att[:, k:k + 1]), [P, NB, HEADS, HEAD_DIM]), ALU.mult))
                    ch.link(nc.vector.tensor_reduce(score, heads(tmp[:]), AX.X, ALU.add))
                dve.sem_inc(tabled, 1)
                mx = seg[:, :, HEADS:]
                ch.link(nc.vector.tensor_tensor(mx, scores_of(tab[:]), seg[:, :, 0:HEADS], ALU.add))
                ch.link(nc.vector.scalar_tensor_tensor(mx, mx, SLOPE, mx, ALU.mult, ALU.max))
                ch.link(nc.vector.tensor_copy(c["agg"][:], tab[:]))
                ch.link(nc.vector.memset(scores_of(c["agg"][:]), 1.0))


def l3_edges(nc, c, blk, seg, first, fence):
    es = ExitStack()
    sb = lambda shape, dt=F32: es.enter_context(nc.sbuf_tensor(fresh("buf"), shape, dt))
    sem = lambda: es.enter_context(nc.semaphore(fresh("sem")))
    agg, S, R = c["agg"], 2 * HEADS, 4
    K = HALF // 2 * HEADS
    turned = flat(c["tab"][:])
    assert NH % R == 0 and 2 * HALF * P <= NB * W
    with es:
        stage, rows, oh = sb([P, R, HALF], I32), sb([P, R, HALF, W]), sb([P, R, HALF, P])
        ohT16 = sb([P, 2, 4 * P], BF16)
        packed, packedT = sb([P, 2, P]), sb([P, 2, 2, P], BF16)
        pick, bar, picks = sb([P, K, P], BF16), sb([P, P], BF16), sb([P, K])
        part, rest = sb([P, 2, K], BF16), sb([P, 2, K])
        best, now, new = sb([P, PAIRS, HEADS]), sb([P, PAIRS, S]), sb([P, PAIRS, S])
        cand, run, fences = sb([P, HEADS, PAIRS]), sb([P, HEADS, PAIRS]), sb([P, HEADS, PAIRS])
        before = sb([1, NPAIR + PAIRS], I32)
        fall, factor, z = sb([P, PAIRS, HEADS]), sb([P, PAIRS, HEADS]), sb([P, HALF, HEADS])
        psT = es.enter_context(nc.psum_tensor(fresh("psum"), [P, 512], F32))
        psK = es.enter_context(nc.psum_tensor(fresh("psum"), [P, 512], F32))
        psQ = es.enter_context(nc.psum_tensor(fresh("psum"), [P, 2, 2, 512], F32))
        psA = es.enter_context(nc.psum_tensor(fresh("psum"), [P, 2, 512], F32))
        psE = psK[:, 2 * P:2 * P + HALF * S].rearrange("p (t k) -> p t k", k=S)
        (staged, got0, got1, got2, got3, gathering, hot, packs, pack_ps, pack_ready, ohT_ps, ohT_ready, scored, reduced, maxed, cleared, consts,
         splitting, raising, raised, writing, multiplying, weighing, had, renewed, dropping, fell, expanded, zed, weights, weighted, summed_six, summed_two, added) = (sem() for _ in range(34))
        got = (got0, got1, got2, got3)
        sums = lambda q: psA[:, q // 3 % 2, (q % 3) * W:(q % 3 + 1) * W]
        halves_got = lambda i, h: 256 * i + 256 * (h // R + 1)
        first_of = lambda i, h: i * (R * PAIRS) + h * PAIRS
        tile_of = lambda i, h: i * (R * HALF) + h * HALF

        def blocks_of(engine, blk, i, h):
            return nc.values_load_multi_w_load_instructions(
                blk[0:1, bass.ds(first_of(i, h), PAIRS)], engines=[engine], min_val=0, max_val=NB - 1,
                skip_runtime_bounds_check_because=BLOCK_RANGE)[1]

        with nc.Block() as block:
            @block.gpsimd
            def _(pool):
                def gather(m, s):
                    pool.wait_ge(staged, m + 1)
                    pool.sem_inc(gathering, 1)
                    gather_half(nc, pool, c["table"], stage[:, s], rows[:, s], got[s], W)
                def weigh(n, h):
                    pool.wait_ge(weights, n + 1)
                    pool.sem_inc(multiplying, 1)
                    f = features(rows[:, h])
                    nc.gpsimd.tensor_tensor(f, f, bc(heads(rows[:, h])[:, :, :, HEAD_DIM:HW], [P, HALF, HEADS, HEAD_DIM]), ALU.mult).then_inc(weighted, 1)

                pool.sem_inc(weighted, 1)
                for m in range(R - 1):
                    gather(m, m)
                with pool.Fori(0, NH // R) as i:
                    for h in range(R):
                        weigh(R * i + h, h)
                        gather(R * i + (h + 3), (h + 3) % R)

            @block.scalar
            def _(act):
                def turn(m, s, g):
                    act.wait_ge(ohT_ps, 4 * m + (g + 1))
                    if g >= 2:
                        act.wait_ge(scored, 8 * m + 2 * (g - 1))
                    nc.scalar.copy(ohT16[:, g % 2], psT[:])
                    nc.scalar.copy(turned[:, (s % 2 * 4 + g) * 4 * P:(s % 2 * 4 + g + 1) * 4 * P], psT[:]).then_inc(ohT_ready, 1)

                def pack(m, s):
                    act.wait_ge(pack_ps, m + 1)
                    nc.scalar.copy(flat(packedT[:, s % 2]), psK[:, 0:2 * P]).then_inc(pack_ready, 1)

                def have(m, blocks):
                    for q in range(PAIRS):
                        last = nc.scalar.copy(now[:, q, :], flat(seg[:, bass.ds(blocks[q], 1), :]))
                    last.then_inc(had, 1)

                def renew(n, blocks):
                    act.wait_ge(raised, n + 1)
                    for q in range(PAIRS):
                        act.wait_ge(maxed, 8 * n + (q + 1))
                        act.sem_inc(writing, 1)
                        nc.scalar.copy(flat(seg[:, bass.ds(blocks[q], 1), HEADS:]), run[:, :, q]).then_inc(maxed, 1)
                    act.wait_ge(maxed, 8 * n + 9)
                    act.sem_inc(writing, 1)
                    for q in range(PAIRS):
                        last = nc.scalar.copy(new[:, q, :], flat(seg[:, bass.ds(blocks[q], 1), :]))
                    last.then_inc(renewed, 1)

                act.sem_inc(maxed, 1)
                for s in range(R - 1):
                    nc.scalar.copy(stage[:, s], c["idx"][:, s * HALF:(s + 1) * HALF]).then_inc(staged, 1)
                b0 = blocks_of(ENG.Activation, blk, 0, 0)
                pack(0, 0)
                for g in range(4):
                    turn(0, 0, g)
                have(0, b0)
                pack(1, 1)
                turn(1, 1, 0)
                with act.Fori(0, NH // R) as i:
                    blocks = blocks_of(ENG.Activation, blk, i, 0)
                    for h in range(R):
                        n, m, s = R * i + h, R * i + (h + 1), (h + 1) % R
                        turn(m, s, 1)
                        renew(n, blocks)
                        turn(m, s, 2)
                        turn(m, s, 3)
                        act.wait_ge(zed, n + 1)
                        nc.scalar.activation(scores_of(rows[:, h]), z[:], ACT.Exp).then_inc(weights, 1)
                        pack(m + 1, s + 1)
                        turn(m + 1, s + 1, 0)
                        act.wait_ge(fell, n + 1)
                        nc.scalar.activation(factor[:], fall[:], ACT.Exp)
                        blocks = blocks_of(ENG.Activation, blk, i, h + 1)
                        have(m, blocks)
                        act.wait_ge(summed_two, n + 1)
                        nc.scalar.copy(stage[:, (h + 3) % R], c["idx"][:, bass.ds(tile_of(i, h + 3), HALF)]).then_inc(staged, 1)

            @block.tensor
            def _(pe):
                def turn(m, s, g):
                    if g or s:
                        pe.wait_ge(ohT_ready, 4 * m + g)
                    for t in range(4):
                        last = nc.tensor.transpose(psT[:, t * P:(t + 1) * P], oh[:, s % R, 4 * g + t, :], c["ident"][:])
                    last.then_inc(ohT_ps, 1)

                def begin(m, s):
                    pe.wait_ge(packs, m + 1)
                    pe.wait_ge(hot, m + 1)
                    nc.tensor.transpose(psK[:, 0:P], packed[:, 0], c["ident"][:])
                    nc.tensor.transpose(psK[:, P:2 * P], packed[:, 1], c["ident"][:]).then_inc(pack_ps, 1)
                    turn(m, s, 0)

                def score(m, s, g, beginning=False):
                    pe.wait_ge(ohT_ready, 4 * m + (g + 1))
                    for q in (2 * g, 2 * g + 1):
                        if q >= 2 or not beginning:
                            pe.wait_ge(reduced, 8 * m + (q - 1))
                        for k in range(2):
                            t = 2 * q + k
                            o = psQ[:, q % 2, k, :]
                            e = ohT16[:, g % 2, (t % 4) * P:(t % 4 + 1) * P]
                            nc.tensor.matmul(o.rearrange("p (k e) -> p k e", k=HEADS), bar[:], bc(e.unsqueeze(1), [P, HEADS, P]),
                                             start=True, stop=False)
                            for j in range(HEADS):
                                last = nc.tensor.matmul(o[:, j * P:(j + 1) * P], pick[:, (t % 8) * HEADS + j, :], packedT[:, s % 2, t // 8, :],
                                                        start=False, stop=(j == HEADS - 1))
                        last.then_inc(scored, 1)

                def spread(n, h):
                    pe.wait_ge(renewed, n + 1)
                    for t in range(HALF):
                        last = nc.tensor.matmul(psE[:, t, :], turned[:, (h % 2 * HALF + t) * P:(h % 2 * HALF + t + 1) * P],
                                                new[:, t // 2, :], start=True, stop=True)
                    last.then_inc(expanded, 1)

                def total(h, pairs, summed):
                    for q in pairs:
                        for k in range(2):
                            last = nc.tensor.matmul(sums(q), oh[:, h, 2 * q + k, :], rows[:, h, 2 * q + k, :], start=(k == 0), stop=(k == 1))
                    last.then_inc(summed, 1)

                pe.wait_ge(consts, 1)
                begin(0, 0)
                pe.wait_ge(pack_ready, 1)
                for g in range(4):
                    if g < 3:
                        turn(0, 0, g + 1)
                    score(0, 0, g, beginning=True)
                begin(1, 1)
                with pe.Fori(0, NH // R) as i:
                    for h in range(R):
                        n, m, s = R * i + h, R * i + (h + 1), (h + 1) % R
                        turn(m, s, 1)
                        pe.wait_ge(pack_ready, m + 1)
                        score(m, s, 0)
                        pe.wait_ge(weighted, n + 1)
                        pe.wait_ge(added, 16 * n + 1)
                        total((h + 3) % R, range(6), summed_six)
                        turn(m, s, 2)
                        score(m, s, 1)
                        turn(m, s, 3)
                        score(m, s, 2)
                        spread(n, h)
                        pe.wait_ge(added, 16 * n + 7)
                        total((h + 3) % R, (6, 7), summed_two)
                        begin(m + 1, (s + 1) % R + R)
                        score(m, s, 3)
                pe.wait_ge(weighted, NH + 1)
                pe.wait_ge(added, 16 * NH + 1)
                total(R - 1, range(6), summed_six)
                pe.wait_ge(added, 16 * NH + 7)
                total(R - 1, (6, 7), summed_two)

            @block.vector
            def _(dve):
                def split(m, s, rows_at):
                    dve.wait_ge(got[s], rows_at)
                    lp = Chain(dve, splitting, start=m * 5)
                    sc = scores_of(rows[:, s]).rearrange("p (g t) k -> p g t k", g=2)
                    as_t = lambda b: b.rearrange("p g (t k) -> p g t k", k=HEADS)
                    lp.link(nc.vector.tensor_copy(as_t(part[:]), sc))
                    nc.vector.tensor_copy(packed[:, :, 0:K], part[:])
                    lp.link(nc.vector.tensor_tensor(as_t(rest[:]), sc, as_t(part[:]), ALU.subtract))
                    lp.link(nc.vector.tensor_copy(part[:], rest[:]))
                    nc.vector.tensor_copy(packed[:, :, K:2 * K], part[:])
                    lp.link(nc.vector.tensor_tensor(rest[:], rest[:], part[:], ALU.subtract))
                    lp.link(nc.vector.tensor_copy(part[:], rest[:]))
                    nc.vector.tensor_copy(packed[:, :, 2 * K:3 * K], part[:]).then_inc(packs, 1)

                def reduce(m, q):
                    dve.wait_ge(scored, 8 * m + (q + 1))
                    nc.vector.tensor_reduce(best[:, q], psQ[:, q % 2].rearrange("p s (k e) -> p k s e", k=HEADS),
                                            AX.XY, ALU.max).then_inc(reduced, 1)

                def raise_max(m, pair):
                    lp = Chain(dve, raising, start=m * 3)
                    dve.wait_ge(had, m + 1)
                    dve.wait_ge(reduced, 8 * m + 8)
                    nc.vector.tensor_copy(fences[:], bc(fence[:, bass.ds(pair, PAIRS)].unsqueeze(1), [P, HEADS, PAIRS]))
                    lp.link(nc.vector.tensor_tensor(best[:], best[:], now[:, :, 0:HEADS], ALU.add))
                    lp.link(nc.vector.scalar_tensor_tensor(best[:], best[:], SLOPE, best[:], ALU.mult, ALU.max))
                    lp.link(nc.vector.tensor_tensor(cand[:].rearrange("p k q -> p q k"), best[:], now[:, :, HEADS:], ALU.max))
                    nc.vector.tensor_tensor_scan(flat(run[:]), flat(fences[:]), flat(cand[:]), 0.0, ALU.add, ALU.max).then_inc(raised, 1)

                def drop(m, first_pair):
                    dve.wait_ge(renewed, m + 1)
                    lp = Chain(dve, dropping, start=m)
                    lp.link(nc.vector.tensor_tensor(fall[:], now[:, :, HEADS:], new[:, :, HEADS:], ALU.subtract))
                    nc.vector.tensor_tensor(fall[:], fall[:], bc(first[:, bass.ds(first_pair, PAIRS)].unsqueeze(2), [P, PAIRS, HEADS]),
                                            ALU.mult).then_inc(fell, 1)

                def score(n, h):
                    dve.wait_ge(expanded, n + 1)
                    lp = Chain(dve, weighing, start=n * 2)
                    lp.link(nc.vector.tensor_tensor(z[:], psE[:, :, 0:HEADS], scores_of(rows[:, h]), ALU.add))
                    lp.link(nc.vector.scalar_tensor_tensor(z[:], z[:], SLOPE, z[:], ALU.mult, ALU.max))
                    nc.vector.tensor_tensor(z[:], z[:], psE[:, :, HEADS:], ALU.subtract).then_inc(zed, 1)

                def add(n, pairs, blocks):
                    for q in pairs:
                        a = agg[:, bass.ds(blocks[q], 1), :].rearrange("p b (h k) -> p (b h) k", h=HEADS)
                        dve.wait_ge(added, 16 * n + (2 * q + 1))
                        nc.vector.tensor_tensor(a, a, bc(factor[:, q, :].unsqueeze(2), [P, HEADS, HW]), ALU.mult).then_inc(added, 1)
                        dve.wait_ge(added, 16 * n + (2 * q + 2))
                        nc.vector.tensor_tensor(a, a, sums(q).rearrange("p (h k) -> p h k", h=HEADS), ALU.add).then_inc(added, 1)

                nc.vector.memset(packed[:], 0.0).then_inc(cleared, 1)
                dve.wait_ge(cleared, 1)
                ch = Chain(dve, cleared, start=1)
                ch.link(nc.vector.tensor_tensor(picks[:], c["ident"][:, 0:K], c["ident"][:, K:2 * K], ALU.add))
                ch.link(nc.vector.tensor_tensor(picks[:], picks[:], c["ident"][:, 2 * K:3 * K], ALU.add))
                ch.link(nc.vector.tensor_copy(pick[:], bc(picks[:].unsqueeze(2), [P, K, P])))
                nc.vector.tensor_scalar(bar[:], c["ident"][:], -1.0, BIG, ALU.add, ALU.mult).then_inc(consts, 1)
                dve.sem_inc(added, 1)
                nc.vector.memset(factor[:], 1.0)
                nc.vector.memset(rows[:, R - 1], 0.0)
                nc.vector.memset(oh[:, R - 1], 0.0)
                ch.link(nc.vector.memset(before[:], 0))
                ch.link(nc.vector.tensor_copy(before[:, PAIRS:], blk[:, 0:NPAIR]))
                onehot(nc, c, oh[:, 0], 0).then_inc(hot, 1)
                onehot(nc, c, oh[:, 1], HALF).then_inc(hot, 1)
                split(0, 0, 256)
                for q in range(PAIRS):
                    reduce(0, q)
                split(1, 1, 256)
                raise_max(0, 0)
                with dve.Fori(0, NH // R) as i:
                    for h in range(R):
                        n, m, s = R * i + h, R * i + (h + 1), (h + 1) % R
                        blocks = blocks_of(ENG.DVE, before, i, h)
                        onehot(nc, c, oh[:, (h + 2) % R], tile_of(i, h + 2)).then_inc(hot, 1)
                        reduce(m, 0)
                        reduce(m, 1)
                        dve.wait_ge(summed_six, n + 1)
                        add(n, range(3), blocks)
                        reduce(m, 2)
                        reduce(m, 3)
                        add(n, range(3, 6), blocks)
                        reduce(m, 4)
                        reduce(m, 5)
                        score(n, h)
                        split(m + 1, (h + 2) % R, halves_got(i, h + 2))
                        dve.wait_ge(summed_two, n + 1)
                        add(n, (6, 7), blocks)
                        drop(n, first_of(i, h))
                        reduce(m, 6)
                        reduce(m, 7)
                        raise_max(m, first_of(i, h + 1))
                dve.wait_ge(summed_six, NH + 1)
                last = blocks_of(ENG.DVE, blk, NH // R - 1, R - 1)
                add(NH, range(6), last)
                dve.wait_ge(summed_two, NH + 1)
                add(NH, (6, 7), last)


def l3_finish(nc, c, ins):
    agg, x = c["agg"], c["x"]
    with (nc.sbuf_tensor("l3_bias", [P, D], F32) as bias, nc.sbuf_tensor("l3_inverse", [P, NB, HEADS], F32) as inv,
          nc.semaphore("l3_loaded") as loaded, nc.semaphore("l3_chain") as dve_chain, nc.Block() as block):
        @block.sync
        def _(sp):
            sp.dma_start(bias[:], row_of(ins["L3_gnn_bias"]).broadcast_to([P, D])).then_inc(loaded, 16)

        @block.vector
        def _(dve):
            ch = Chain(dve, dve_chain)
            ch.link(nc.vector.reciprocal(inv[:], scores_of(agg[:])))
            sums = features(agg[:])
            ch.link(nc.vector.tensor_tensor(sums, sums, bc(inv[:].unsqueeze(3), [P, NB, HEADS, HEAD_DIM]), ALU.mult))
            ch.link(nc.vector.tensor_tensor(heads(x[:]), heads(x[:]), sums, ALU.add))
            dve.wait_ge(loaded, 16)
            ch.link(nc.vector.tensor_tensor(x[:], x[:], bc(bias[:].unsqueeze(1), [P, NB, D]), ALU.add))


_INS = ["x", "src", "dst", "edge_attr_128", "L0_gnn_W_w", "L0_gnn_W_b", "L0_gnn_a_w", "L0_gnn_a_b", "L1_gnn_ln_gamma",
        "L1_gnn_ln_beta", "L1_gnn_phi_w1", "L1_gnn_phi_b1", "L1_gnn_phi_w2", "L1_gnn_phi_b2", "L1_gnn_theta_w",
        "L1_gnn_theta_b", "L2_gnn_Wl", "L2_gnn_bl", "L2_gnn_Wr", "L2_gnn_br", "L3_gnn_W", "L3_gnn_att_src",
        "L3_gnn_att_dst", "L3_gnn_bias"]


def kernel(**inputs):
    import numpy as np
    import concourse.bacc as bacc
    from concourse.bass_utils import run_bass_kernel_spmd as run

    nc = bacc.Bacc("TRN2", target_bir_lowering=False, num_devices=1)
    arrays, aps = {}, {}
    for name in _INS:
        a = np.ascontiguousarray(inputs[name])
        arrays[f"in_{name}"] = a
        aps[name] = nc.dram_tensor(f"in_{name}", a.shape, mybir.dt.from_np(a.dtype), kind="ExternalInput").ap()
    out = nc.dram_tensor("out_x", (N, D), F32, kind="ExternalOutput").ap()
    gnn_kernel(nc, aps, out)
    r = run(nc, [arrays], core_ids=[0])
    return r.results[0]["out_x"]
```
